# Optimizing a Trainium2 kernel written in Bass

```python
import numpy as np
import jax
import jax.numpy as jnp

def _softmax(x, axis=-1):
    return jax.nn.softmax(x, axis=axis)
def _gelu(x):
    return jax.nn.gelu(x, approximate=True)
def _silu(x):
    return jax.nn.silu(x)
def _sigmoid(x):
    return jax.nn.sigmoid(x)
def _layernorm(x, axis=-1, eps=1e-5):
    m = jnp.mean(x, axis=axis, keepdims=True)
    v = jnp.var(x, axis=axis, keepdims=True)
    return (x - m) / jnp.sqrt(v + eps)
def _scatter_add(tgt, idx, src, axis=0):
    return tgt.at[idx].add(src)
def _segment_sum(src, seg, n):
    return jax.ops.segment_sum(src, seg, n)

kernel_name = 'mk_conv_seq_d2_conv_nchw512_367a32'

def setup_inputs(seed: int = 0):
    np.random.seed(seed)
    _w = jnp.asarray
    def _rec_inputs():
        import jax
        import jax.numpy as jnp
        _gk = jax.random.key(seed)
        x = -0.0002928 + 1 * jax.random.normal(jax.random.fold_in(_gk, 1), (8, 512, 32, 32), jnp.float32)
        return x
    x = _rec_inputs()
    def _L0_conv_setup():
        import jax, jax.numpy as jnp
        import numpy as np
        NHEAD = 8
        GROUPS = 32
        EPS = 1e-05

        def group_norm(x, scale, bias):
            b, c, h, w = x.shape
            xg = x.reshape(b, GROUPS, c // GROUPS, h, w)
            mu = xg.mean(axis=(2, 3, 4), keepdims=True)
            var = xg.var(axis=(2, 3, 4), keepdims=True)
            xg = (xg - mu) * jax.lax.rsqrt(var + EPS)
            return xg.reshape(b, c, h, w) * scale[None, :, None, None] + bias[None, :, None, None]
        key = jax.random.key(seed)
        ks = jax.random.split(key, 3)
        B, C, H, W = (8, 512, 32, 32)
        s = 0.02
        return {'x': jax.random.normal(ks[0], (B, C, H, W), jnp.float32), 'gn1_scale': jnp.ones((C,), jnp.float32), 'gn1_bias': jnp.zeros((C,), jnp.float32), 'w_qkv': jax.random.normal(ks[1], (3 * C, C), jnp.float32) * s, 'b_qkv': jnp.zeros((3 * C,), jnp.float32), 'w_proj': jax.random.normal(ks[2], (C, C), jnp.float32) * s, 'b_proj': jnp.zeros((C,), jnp.float32), 'gn2_scale': jnp.ones((C,), jnp.float32), 'gn2_bias': jnp.zeros((C,), jnp.float32)}
    _L0_conv_all = _L0_conv_setup()
    _L0_conv_in = {k: v for k, v in _L0_conv_all.items() if k in ('gn1_scale', 'gn1_bias', 'w_qkv', 'b_qkv', 'w_proj', 'b_proj', 'gn2_scale', 'gn2_bias', )}
    del _L0_conv_all

    def _L1_conv_setup():
        import jax, jax.numpy as jnp
        import numpy as np

        def _weight_norm(v, g):
            return g[:, None] * v / jnp.linalg.norm(v, axis=1, keepdims=True)
        key = jax.random.key(seed)
        k0, k1, k2 = jax.random.split(key, 3)
        B, C, H, W = (4, 512, 64, 64)
        x = jax.random.normal(k0, (B, C, H, W), dtype=jnp.float32)
        v_qkv = jax.random.normal(k1, (3 * C, C), dtype=jnp.float32) * 0.02
        g_qkv = jnp.ones((3 * C,), dtype=jnp.float32)
        v_out = jax.random.normal(k2, (C, C), dtype=jnp.float32) * 0.02
        g_out = jnp.ones((C,), dtype=jnp.float32)
        return {'x': x, 'v_qkv': v_qkv, 'g_qkv': g_qkv, 'v_out': v_out, 'g_out': g_out}
    _L1_conv_all = _L1_conv_setup()
    _L1_conv_in = {k: v for k, v in _L1_conv_all.items() if k in ('v_qkv', 'g_qkv', 'v_out', 'g_out', )}
    del _L1_conv_all

    return {
        "x": x,
        "L0_conv_gn1_scale": _L0_conv_in["gn1_scale"],
        "L0_conv_gn1_bias": _L0_conv_in["gn1_bias"],
        "L0_conv_w_qkv": _L0_conv_in["w_qkv"],
        "L0_conv_b_qkv": _L0_conv_in["b_qkv"],
        "L0_conv_w_proj": _L0_conv_in["w_proj"],
        "L0_conv_b_proj": _L0_conv_in["b_proj"],
        "L0_conv_gn2_scale": _L0_conv_in["gn2_scale"],
        "L0_conv_gn2_bias": _L0_conv_in["gn2_bias"],
        "L1_conv_v_qkv": _L1_conv_in["v_qkv"],
        "L1_conv_g_qkv": _L1_conv_in["g_qkv"],
        "L1_conv_v_out": _L1_conv_in["v_out"],
        "L1_conv_g_out": _L1_conv_in["g_out"],
    }

def reference(x, L0_conv_gn1_scale, L0_conv_gn1_bias, L0_conv_w_qkv, L0_conv_b_qkv, L0_conv_w_proj, L0_conv_b_proj, L0_conv_gn2_scale, L0_conv_gn2_bias, L1_conv_v_qkv, L1_conv_g_qkv, L1_conv_v_out, L1_conv_g_out):
    import jax
    import jax.numpy as jnp
    def _L0_conv_ref(x, gn1_scale, gn1_bias, w_qkv, b_qkv, w_proj, b_proj, gn2_scale, gn2_bias):
        import jax, jax.numpy as jnp
        import numpy as np
        NHEAD = 8
        GROUPS = 32
        EPS = 1e-05

        def group_norm(x, scale, bias):
            b, c, h, w = x.shape
            xg = x.reshape(b, GROUPS, c // GROUPS, h, w)
            mu = xg.mean(axis=(2, 3, 4), keepdims=True)
            var = xg.var(axis=(2, 3, 4), keepdims=True)
            xg = (xg - mu) * jax.lax.rsqrt(var + EPS)
            return xg.reshape(b, c, h, w) * scale[None, :, None, None] + bias[None, :, None, None]
        b, c, h, w = x.shape
        n = h * w
        ch = c // NHEAD
        hn = group_norm(x, gn1_scale, gn1_bias)
        qkv = jnp.einsum('bchw,oc->bohw', hn, w_qkv) + b_qkv[None, :, None, None]
        qkv = qkv.reshape(b * NHEAD, 3 * ch, n)
        q, k, v = jnp.split(qkv, 3, axis=1)
        scale = ch ** (-0.25)
        wgt = jnp.einsum('bct,bcs->bts', q * scale, k * scale)
        wgt = jax.nn.softmax(wgt, axis=-1)
        a = jnp.einsum('bts,bcs->bct', wgt, v).reshape(b, c, h, w)
        out = jnp.einsum('bchw,oc->bohw', a, w_proj) + b_proj[None, :, None, None]
        out = group_norm(out, gn2_scale, gn2_bias)
        return x + out

    def _L1_conv_ref(x, v_qkv, g_qkv, v_out, g_out):
        import jax, jax.numpy as jnp
        import numpy as np

        def _weight_norm(v, g):
            return g[:, None] * v / jnp.linalg.norm(v, axis=1, keepdims=True)
        B, C, H, W = x.shape
        w_qkv = _weight_norm(v_qkv, g_qkv)
        w_out = _weight_norm(v_out, g_out)
        xt = x.reshape(B, C, H * W)
        qkv = jnp.einsum('oc,bcn->bon', w_qkv, xt)
        rms = jnp.sqrt(jnp.mean(jnp.square(qkv), axis=1, keepdims=True)) + 0.0001
        qkv = qkv / rms
        q, k, v = jnp.split(qkv, 3, axis=1)
        scores = jnp.einsum('bci,bcj->bij', q, k) * C ** (-0.5)
        attn = jax.nn.softmax(scores, axis=-1)
        h = jnp.einsum('bij,bcj->bci', attn, v)
        h = jnp.einsum('oc,bcn->bon', w_out, h).reshape(B, C, H, W)
        return (x + h) * 2.0 ** (-0.5)

    def _gn(v, G=32, eps=1e-5):
        B_, C_, H_, W_ = v.shape
        g = v.reshape(B_, G, C_ // G, H_, W_)
        m = jnp.mean(g, axis=(2, 3, 4), keepdims=True)
        s = jnp.var(g, axis=(2, 3, 4), keepdims=True)
        return ((g - m) / jnp.sqrt(s + eps)).reshape(v.shape)

    def _ln_c(v, eps=1e-6):
        m = jnp.mean(v, axis=1, keepdims=True)
        s = jnp.var(v, axis=1, keepdims=True)
        return (v - m) / jnp.sqrt(s + eps)

    def _ln_t(v, eps=1e-5):
        m = jnp.mean(v, axis=-1, keepdims=True)
        s = jnp.var(v, axis=-1, keepdims=True)
        return (v - m) / jnp.sqrt(s + eps)

    def _to_tokens(v):
        B_, C_, H_, W_ = v.shape
        return v.reshape(B_, C_, H_ * W_).transpose(0, 2, 1)
    def _from_tokens(t, like):
        B_, C_, H_, W_ = like.shape
        return t.transpose(0, 2, 1).reshape(B_, C_, H_, W_)

    x = _L0_conv_ref(x, L0_conv_gn1_scale, L0_conv_gn1_bias, L0_conv_w_qkv, L0_conv_b_qkv, L0_conv_w_proj, L0_conv_b_proj, L0_conv_gn2_scale, L0_conv_gn2_bias)
    x = _L1_conv_ref(x, L1_conv_v_qkv, L1_conv_g_qkv, L1_conv_v_out, L1_conv_g_out)
    return x


_drawn_inputs = setup_inputs


def setup_inputs(seed=0):
    import zlib

    import numpy as np

    out = dict(_drawn_inputs(seed))
    spreads = {'L0_conv_gn1_scale': (1.0, 0.6),
     'L0_conv_gn1_bias': (0.0, 0.1),
     'L0_conv_b_qkv': (0.0, 0.1),
     'L0_conv_b_proj': (0.0, 0.1),
     'L0_conv_gn2_scale': (1.0, 0.2),
     'L0_conv_gn2_bias': (0.0, 0.1),
     'L1_conv_g_qkv': (1.0, 0.2),
     'L1_conv_g_out': (1.0, 0.2)}
    factors = {}
    for name, (base, spread) in spreads.items():
        noise = np.random.default_rng([zlib.crc32(name.encode()), seed]).standard_normal(out[name].shape)
        drawn = base * np.exp(spread * noise) if base else spread * noise
        out[name] = jnp.asarray(drawn.astype(out[name].dtype))
    for name, factor in factors.items():
        out[name] = (out[name] * factor).astype(out[name].dtype)
    return out
```

```python
import concourse.bass as bass
from concourse import mybir
from contextlib import ExitStack

B, C, N = 8, 512, 1024
HEADS = 8
CH = C // HEADS
P = 128
KB = C // P
NT = N // P
HALF = 512
PAIRS = HEADS // 2
UNITS0 = HEADS * 2
UNITS = UNITS0 + 2
GN_EPS = 1e-5
RMS_EPS = 1e-4
RES = 2.0 ** -0.5

f32 = mybir.dt.float32
f32r = mybir.dt.float32r
ACT = mybir.ActivationFunctionType
ALU = mybir.AluOpType
AX = mybir.AxisListType

BIG = [("v", s) for s in range(4)] + [("qk", 0), ("qk", 1)] + [("v", s) for s in range(4, NT)]
for _u in range(UNITS0):
    if _u % 4 < 2 and _u // 4 + 1 < PAIRS:
        BIG.append(("qk", 2 * (_u // 4 + 1) + _u % 4))
    BIG += [("s", 4 * _u + t) for t in range(4)]
BIG += [("proj", k) for k in range(KB)] + [("gna", 0), ("gnb", 0)] + [("g", k) for k in range(KB)]
BIG += [("y", 0), ("sum", 0), ("y", 1), ("y", 2), ("r", 0), ("y", 3)] + [("u", s) for s in range(NT)]
BIG += [("s1", t) for t in range(8)] + [("gna", 1), ("gnb", 1)]
NBIG = len(BIG)
assert NBIG % 2 == 0
HI = [key for key in BIG if key[0] in ("v", "qk", "y", "u")]
BIG_AT = {name: i for i, name in enumerate(BIG)}
SETUP_BIG = 3 * KB
BIG_BASE = SETUP_BIG + 2
DVE_LINKS = 23
SCALE0 = float(CH) ** -0.5
SCALE1 = float(C) ** -0.5
STEPS0 = 4 * UNITS0
LAG = 5
CREDIT = 1


def build(nc, x, wv_t, wp_t, wqk_t, v_qkv, v_out, wo_t, vecs, consts, out):
    ctx = ExitStack()
    with ctx:
        def sb(name, shape, dt=f32):
            return ctx.enter_context(nc.sbuf_tensor(name, shape, dt))

        def ps(name, cols):
            return ctx.enter_context(nc.psum_tensor(name, [P, cols], f32))

        def sem(name):
            return ctx.enter_context(nc.semaphore(name))

        d_wv = nc.dram_tensor("d_wv", [P, 4096], f32)
        d_wp = nc.dram_tensor("d_wp", [P, 4096], f32)
        d_qk = nc.dram_tensor("d_qk", [PAIRS, P, 2048], f32)
        d_g = nc.dram_tensor("d_g", [P, 4096], f32)
        d_m = nc.dram_tensor("d_m", [P, 4096], f32)
        d_u = nc.dram_tensor("d_u", [P, 4096], f32)

        X = sb("X", [P, KB, N])
        XA = sb("XA", [P, KB, N])
        HH = sb("HH", [P, KB, N], f32r)
        HL = sb("HL", [P, KB, N], f32r)
        VT = sb("VT", [P, NT, N], f32r)
        ST = sb("ST", [P, 10, N], f32r)
        PB = sb("PB", [P, 8, N])
        PT = sb("PT", [P, 4, 2, HALF], f32r)
        W = [sb("W0", [P, 4096], f32r), sb("W1", [P, 4096], f32r)]
        RB = sb("RB", [P, N])
        ident = sb("ident", [P, P])
        gavg = sb("gavg", [P, P])
        ones = sb("ones", [P, P])
        vec = sb("vec", [P, 48])
        small = sb("small", [P, 208])
        stats = small[:, 0:48].rearrange("p (k s) -> p k s", k=KB)
        mv = small[:, 48:56].rearrange("p (k s) -> p k s", k=KB)
        gmean, dev, wvar = small[:, 56:60], small[:, 60:64], small[:, 64:68]
        veps, rstd, coefA = small[:, 68:72], small[:, 72:76], small[:, 76:80]
        coefT, coefB = small[:, 80:84], small[:, 84:88]
        negmax, rowsum, rinv = small[:, 88:96], small[:, 96:104], small[:, 104:112]
        mean_sq, rms, rcol = small[:, 112:120], small[:, 120:128], small[:, 128:136]
        rowmax1 = small[:, 136:144]
        ssq, rnorm, wscale = small[:, 144:160], small[:, 160:176], small[:, 176:192]
        expo = small[:, 192:208]
        bq, bk, bv = vec[:, 0:4], vec[:, 4:8], vec[:, 8:12]
        gs1, gb1, gs2, gb2, bp = (vec[:, 12 + 4 * i:16 + 4 * i] for i in range(5))
        g_l1 = vec[:, 32:48]

        big = [ps("big0", N), ps("big1", N)]
        tps = [ps("tps0", HALF), ps("tps1", HALF)]
        ops = [ps("ops0", HALF), ps("ops1", HALF)]

        PT1 = W[1][:, :].rearrange("p (s h n) -> p s h n", s=4, h=2)

        def pt_slot(u, s):
            if u < UNITS0:
                return PT[:, s % 4, :, :]
            return PT[:, s, :, :] if s < 4 else PT1[:, s - 4, :, :]

        def stack(kind, head):
            return ST[:, {"q": 0, "kh": 2, "kl": 4}[kind] + head, :]

        def unstacked(kind, part):
            return ST[:, 6 + 2 * kind + part, :]

        w_full = [w[:, :].rearrange("p (h k n) -> p h k n", h=2, k=KB) for w in W]

        def w_qk(pair):
            w = W[1 if pair < 2 else 0][:, 2048 * (pair % 2):2048 * (pair % 2) + 2048]
            return w.rearrange("p (h k n) -> p h k n", h=2, k=KB)

        s_waited = sem("waited")
        s_q_scaled = sem("q_scaled")
        s_in_l0 = sem("in_l0")
        s_in_l1 = sem("in_l1")
        s_in_vout = sem("in_vout")
        s_in_vec = sem("in_vec")
        s_split_hi = sem("split_hi")
        s_split_lo = sem("split_lo")
        s_stored_l0 = sem("stored_l0")
        s_square_sum = sem("square_sum")
        s_norm_pow = sem("norm_pow")
        s_w_normed = sem("w_normed")
        s_prod_hi = sem("prod_hi")
        s_prod_lo = sem("prod_lo")
        s_stored_l1 = sem("stored_l1")
        s_dve_step = sem("dve_step")
        s_const_set = sem("const_set")
        s_x_next = sem("x_next")
        s_x_res = sem("x_res")
        s_ld_wv = sem("ld_wv")
        s_ld_wp = sem("ld_wp")
        s_ld_g = sem("ld_g")
        s_ld_m = sem("ld_m")
        s_ld_u = sem("ld_u")
        s_stack_a = sem("stack_a")
        s_stack_b = sem("stack_b")
        s_out_done = sem("out_done")
        s_big_full = sem("big_full")
        s_big_hi = sem("big_hi")
        s_v_ready = sem("v_ready")
        s_nat_ready = sem("nat_ready")
        s_t_full = sem("t_full")
        s_pt_hi = sem("pt_hi")
        s_pt_ready = sem("pt_ready")
        s_o_full = sem("o_full")
        s_row_max = sem("row_max")
        s_exp_done = sem("exp_done")
        s_recip_done = sem("recip_done")
        s_p_norm = sem("p_norm")
        s_corr_done = sem("corr_done")
        s_a_done = sem("a_done")
        s_a_hi = sem("a_hi")
        s_a_lo = sem("a_lo")
        s_pr_ready = sem("pr_ready")
        s_gn_mean = sem("gn_mean")
        s_gn_var = sem("gn_var")
        s_gn_veps = sem("gn_veps")
        s_gn_rstd = sem("gn_rstd")
        s_res_sum = sem("res_sum")
        s_xc_ready = sem("xc_ready")
        s_xc_hi = sem("xc_hi")
        s_xc_lo = sem("xc_lo")
        s_prod_ready = sem("prod_ready")
        s_ms_done = sem("ms_done")
        s_rms_done = sem("rms_done")
        s_diag_ready = sem("diag_ready")
        s_r_ready = sem("r_ready")
        s_y_ready = sem("y_ready")
        s_vp_ready = sem("vp_ready")
        s_s1_ready = sem("s1_ready")
        s_neg_ready = sem("neg_ready")
        s_hn_f = sem("hn_f")
        s_hn_hi = sem("hn_hi")
        s_hn_ready = sem("hn_ready")
        s_y_out = sem("y_out")
        ld_qk = [sem(f"ld_qk{i}") for i in range(PAIRS)]
        block = ctx.enter_context(nc.Block())

        def each_batch(eng, body):
            with eng.Fori(0, B - 1) as b:
                body(b, False)
            body(B - 1, True)

        def big_count(b, key):
            return BIG_BASE + b * NBIG + BIG_AT[key] + 1

        def hi_count(b, key):
            return b * len(HI) + HI.index(key) + 1

        def own_wait(eng):
            eng.sem_inc(s_waited, 1)

        def src_x(b):
            return x[b].rearrange("(k p) n -> p k n", p=P)

        @block.sync
        def _(sp):
            sp.sem_inc(s_out_done, 16 * CREDIT)
            sp.dma_start(vec[:], vecs).then_inc(s_in_vec, 16)
            sp.dma_start(ident[:], consts[0]).then_inc(s_in_vec, 16)
            sp.dma_start(gavg[:], consts[1]).then_inc(s_in_vec, 16)
            for j in range(12):
                sp.dma_start(PB[:, j // 2, HALF * (j % 2):HALF * (j % 2 + 1)], v_qkv[j]).then_inc(s_in_l1, 16)
            sp.dma_start(PB[:, 6:8, :].rearrange("p a n -> p (a n)"), wo_t).then_inc(s_in_l1, 16)
            sp.dma_start(XA[:, 0:2, :].rearrange("p a n -> p (a n)"), v_out).then_inc(s_in_vout, 16)
            sp.dma_start(X[:, 0:2, :].rearrange("p a n -> p (a n)"), wv_t).then_inc(s_in_l0, 16)
            sp.dma_start(X[:, 2:4, :].rearrange("p a n -> p (a n)"), wp_t).then_inc(s_in_l0, 16)
            for i in range(2):
                sp.dma_start(XA[:, 2 + i, :], wqk_t[i]).then_inc(s_in_l0, 16)
            sp.wait_ge(s_square_sum, 16)
            for i in range(2):
                sp.dma_start(XA[:, i, :], wqk_t[2 + i]).then_inc(s_in_l0, 16)
            sp.wait_ge(s_split_lo, 6)
            sp.dma_start(d_wv[:], W[0][:].bitcast(f32)).then_inc(s_stored_l0, 16)
            sp.dma_start(d_wp[:], W[1][:].bitcast(f32)).then_inc(s_stored_l0, 16)
            for i in range(PAIRS):
                sp.dma_start(d_qk[i], VT[:, 2 * i:2 * i + 2, :].rearrange("p a n -> p (a n)").bitcast(f32))\
                  .then_inc(s_stored_l0, 16)
            sp.dma_start(XA[:], src_x(0)).then_inc(s_x_next, 16)
            for i, (dst, src) in enumerate(((d_g, HH[:, :, :]), (d_m, HL[:, :, :]), (d_u, ST[:, 0:4, :]))):
                sp.wait_ge(s_prod_lo, KB * (i + 1))
                sp.dma_start(dst[:], src.rearrange("p a n -> p (a n)").bitcast(f32)).then_inc(s_stored_l1, 16)
            sp.wait_ge(s_stored_l0, 96)
            sp.wait_ge(s_stored_l1, 48)
            sp.dma_start(W[0][:].bitcast(f32), d_wv[:]).then_inc(s_ld_wv, 16)

            def stack_head(b, pair, head):
                rows = slice(64 * head, 64 * head + 64)
                s_stack = (s_stack_a, s_stack_b)[head]
                sp.wait_ge(s_nat_ready, b * 8 + 2 * pair + 2)
                own_wait(sp)
                if pair:
                    sp.wait_ge(s_big_full, big_count(b, ("s", 16 * (pair - 1) + 8 * head + 7)))
                    own_wait(sp)
                moves = [("q", 64 * head, 0, 0), ("q", 64 - 64 * head, 0, 1)]
                moves += [("kh", q, 1, 0) for q in (0, 64)] + [("kl", q, 1, 1) for q in (0, 64)]
                for kind, to, what, part in moves:
                    sp.dma_start(stack(kind, head)[to:to + 64, :].bitcast(f32),
                                 unstacked(what, part)[rows, :].bitcast(f32))\
                      .then_inc(s_stack, 16)

            def body(b, last):
                sp.wait_ge(s_o_full, b * 24 + CREDIT)
                own_wait(sp)
                for i in (0, 1):
                    sp.dma_start(w_qk(i).rearrange("p h k n -> p (h k n)").bitcast(f32), d_qk[i]).then_inc(ld_qk[i], 16)
                stack_head(b, 0, 0)
                stack_head(b, 0, 1)
                sp.wait_ge(s_out_done, (b * 8 + CREDIT) * 16)
                own_wait(sp)
                sp.dma_start(X[:], src_x(b)).then_inc(s_x_res, 16)
                sp.wait_ge(s_big_full, big_count(b, ("v", NT - 1)))
                own_wait(sp)
                for i in (2, 3):
                    sp.dma_start(w_qk(i).rearrange("p h k n -> p (h k n)").bitcast(f32), d_qk[i]).then_inc(ld_qk[i], 16)
                stack_head(b, 1, 0)
                sp.dma_start(W[1][:].bitcast(f32), d_wp[:]).then_inc(s_ld_wp, 16)
                stack_head(b, 1, 1)
                stack_head(b, 2, 0)
                stack_head(b, 2, 1)
                stack_head(b, 3, 0)
                sp.dma_start(W[0][:].bitcast(f32), d_g[:]).then_inc(s_ld_g, 16)
                stack_head(b, 3, 1)
                sp.wait_ge(s_big_full, big_count(b, ("proj", KB - 1)))
                own_wait(sp)
                sp.dma_start(W[1][:].bitcast(f32), d_m[:]).then_inc(s_ld_m, 16)
                if not last:
                    sp.wait_ge(s_xc_ready, b * KB + KB)
                    own_wait(sp)
                    sp.dma_start(XA[:], src_x(b + 1)).then_inc(s_x_next, 16)
                sp.wait_ge(s_big_full, big_count(b, ("g", KB - 1)))
                own_wait(sp)
                sp.dma_start(W[0][:].bitcast(f32), d_u[:]).then_inc(s_ld_u, 16)
                if not last:
                    sp.wait_ge(s_big_full, big_count(b, ("u", NT - 1)))
                    own_wait(sp)
                    sp.dma_start(W[0][:].bitcast(f32), d_wv[:]).then_inc(s_ld_wv, 16)
                for j in range(8):
                    sp.wait_ge(s_y_out, b * 8 + j + 1 + CREDIT)
                    own_wait(sp)
                    c, e = j // 4, j % 4
                    sp.dma_start(out[b].rearrange("(k p) n -> p k n", p=P)[:, e, HALF * c:HALF * c + HALF],
                                 X[:, e, HALF * c:HALF * c + HALF]).then_inc(s_out_done, 16)

            each_batch(sp, body)
            sp.wait_ge(s_out_done, (B * 8 + CREDIT) * 16)

        @block.tensor
        def _(pe):
            mm = nc.tensor.matmul

            def split_product(dst, stat, mov, ks):
                n, i = 3 * len(ks), 0
                for k in ks:
                    for sp_, mp_ in ((0, 0), (0, 1), (1, 0)):
                        last = mm(dst, stat(sp_, k), mov(mp_, k), start=(i == 0), stop=(i == n - 1))
                        i += 1
                return last

            def w1_block(j, cols=slice(0, HALF)):
                return PB[:, j // 2, HALF * (j % 2) + cols.start:HALF * (j % 2) + cols.stop]

            def setup_tile(i):
                if i >= 2:
                    pe.wait_ge(s_prod_lo, i - 1)
                return big[i % 2][:, 0:HALF]

            pe.sem_inc(s_o_full, CREDIT)
            pe.wait_ge(s_w_normed, 12)
            for i in range(KB):
                t = setup_tile(i)
                for j in range(12):
                    last = mm(t, w1_block(j, slice(P * i, P * i + P)), w1_block(j), start=(j == 0), stop=(j == 11))
                last.then_inc(s_big_full, 1)
            for i in range(KB):
                t = setup_tile(KB + i)
                for j in range(4):
                    last = mm(t, w1_block(j, slice(P * i, P * i + P)), w1_block(4 + j), start=(j == 0), stop=(j == 3))
                last.then_inc(s_big_full, 1)
            for i in range(KB):
                t = setup_tile(2 * KB + i)
                for j in range(4):
                    last = mm(t, w1_block(8 + j, slice(P * i, P * i + P)),
                              PB[:, 6 + j // 2, HALF * (j % 2):HALF * (j % 2 + 1)], start=(j == 0), stop=(j == 3))
                last.then_inc(s_big_full, 1)

            def group_means(n, tile, operand, ready):
                pe.wait_ge(ready, n)
                mm(tile[:, 0:KB], gavg[:], operand, start=True, stop=True).then_inc(s_big_full, 1)

            pe.wait_ge(s_const_set, 1)
            pe.wait_ge(s_in_vec, 48)
            pe.wait_ge(s_prod_lo, SETUP_BIG)
            group_means(1, big[0], mv[:, :, 0], s_gn_mean)
            group_means(1, big[1], wvar, s_gn_var)

            def body(b, last_batch):
                def released(key):
                    i = BIG_AT[key]
                    if i >= 2:
                        kind, k = BIG[i - 2]
                        reader, per = {"v": (s_v_ready, 8), "qk": (s_nat_ready, 8), "s": (s_exp_done, 72),
                                       "proj": (s_pr_ready, 4), "gna": (s_gn_var, 2), "gnb": (s_gn_veps, 2),
                                       "g": (s_prod_ready, 4), "sum": (s_ms_done, 1), "r": (s_r_ready, 1),
                                       "y": (s_y_ready, 4), "u": (s_vp_ready, 8), "s1": (s_s1_ready, 8)}[kind]
                        pe.wait_ge(reader, b * per + k + (2 if kind in ("gna", "gnb") else 1))
                    else:
                        pe.wait_ge(s_gn_veps, 2 * b + 1)
                    return big[i % 2]

                pe.wait_ge(s_hn_ready, b * KB + KB)
                pe.wait_ge(s_ld_wv, b * 16 + 16)
                def project_v(s):
                    t = released(("v", s))
                    split_product(t[:, 0:HALF], lambda h, k: (HH, HL)[h][:, k, P * s:P * s + P],
                                  lambda h, k: w_full[0][:, h, k, :], range(KB)).then_inc(s_big_full, 1)

                def project_qk(j):
                    pair, what = j // 2, j % 2
                    if what == 0:
                        pe.wait_ge(ld_qk[pair], b * 16 + 16)
                    t = released(("qk", j))
                    for half in range(2):
                        cols = slice(HALF * half, HALF * half + HALF)
                        last = split_product(t[:, cols], lambda h, k: w_qk(pair)[:, h, k, P * what:P * what + P],
                                             lambda h, k: (HH, HL)[h][:, k, cols], range(KB))
                    last.then_inc(s_big_full, 1)

                def transposes(u, s):
                    n = 8 * u + s
                    if s == 0:
                        pe.wait_ge(s_p_norm, b * 72 + 4 * u + 4)
                    if n >= 2:
                        pe.wait_ge(s_pt_ready, b * 144 + n - 1)
                    for t in range(4):
                        last = nc.tensor.transpose(tps[n % 2][:, P * t:P * t + P],
                                                   PB[:, 4 * (u % 2) + t, P * s:P * s + P], ident[:])
                    last.then_inc(s_t_full, 1)

                def values0(n):
                    u, s = n // 8, n % 8
                    if s == 0:
                        if u == 0:
                            pe.wait_ge(s_v_ready, b * 8 + 8)
                            pe.wait_ge(s_y_out, b * 8 + CREDIT)
                        elif u == 1:
                            pe.wait_ge(s_y_out, b * 8 + CREDIT)
                        else:
                            pe.wait_ge(s_a_done, b * 16 + u - 1)
                    pe.wait_ge(s_pt_ready, b * 144 + n + 1)
                    for part in range(2):
                        last = mm(ops[u % 2][:], VT[:, s, P * (u // 2):P * (u // 2) + P], pt_slot(u, s)[:, part, :],
                                  start=(s == 0 and part == 0), stop=(s == 7 and part == 1))
                    if s == 7:
                        last.then_inc(s_o_full, 1)

                def scores0(u, tb):
                    head = u // 2 % 2
                    if tb == 0 and u % 2 == 0:
                        pe.wait_ge((s_stack_a, s_stack_b)[head], (b * PAIRS + u // 4 + 1) * 96)
                    t = released(("s", 4 * u + tb))
                    tok = P * (4 * (u % 2) + tb)
                    for half in range(2):
                        cols = slice(HALF * half, HALF * half + HALF)
                        for i, kind in enumerate(("kh", "kl")):
                            last = mm(t[:, cols], stack("q", head)[:, tok:tok + P], stack(kind, head)[:, cols],
                                      start=(i == 0), stop=(i == 1))
                    last.then_inc(s_big_full, 1)

                for s in range(4):
                    project_v(s)
                project_qk(0)
                project_qk(1)
                for s in range(4, NT):
                    project_v(s)
                for step in range(STEPS0 + LAG):
                    u, tb, n = step // 4, step % 4, 2 * (step - LAG)
                    if tb == 0 and u % 4 < 2 and u // 4 + 1 < PAIRS:
                        project_qk(2 * (u // 4 + 1) + u % 4)
                    if step < STEPS0:
                        scores0(u, tb)
                    if n >= 0:
                        transposes(n // 8, n % 8)
                        transposes(n // 8, n % 8 + 1)
                    if n > 0:
                        values0(n - 2)
                        values0(n - 1)
                values0(8 * UNITS0 - 2)
                values0(8 * UNITS0 - 1)

                pe.wait_ge(s_ld_wp, b * 16 + 16)
                pe.wait_ge(s_a_hi, b * 4 + 4)
                pe.wait_ge(s_a_lo, b * 4 + 4)
                for o in range(KB):
                    t = released(("proj", o))
                    for half in range(2):
                        cols = slice(HALF * half, HALF * half + HALF)
                        last = split_product(t[:, cols], lambda h, k: w_full[1][:, h, k, P * o:P * o + P],
                                             lambda h, k: (HH, HL)[h][:, k, cols], range(KB))
                    last.then_inc(s_big_full, 1)
                group_means(2 * b + 2, released(("gna", 0)), mv[:, :, 0], s_gn_mean)
                group_means(2 * b + 2, released(("gnb", 0)), wvar, s_gn_var)

                def from_x1(kind, k, slot):
                    t = released((kind, k))
                    for half in range(2):
                        cols = slice(HALF * half, HALF * half + HALF)
                        last = split_product(t[:, cols], lambda h, j: w_full[slot][:, h, j, P * k:P * k + P],
                                             lambda h, j: (HH, HL)[h][:, j, cols], range(KB))
                    last.then_inc(s_big_full, 1)

                pe.wait_ge(s_ld_g, b * 16 + 16)
                pe.wait_ge(s_xc_lo, b * 4 + 4)
                for k in range(KB):
                    from_x1("g", k, 0)
                pe.wait_ge(s_ld_m, b * 16 + 16)
                from_x1("y", 0, 1)
                t = released(("sum", 0))
                pe.wait_ge(s_prod_ready, b * 4 + 4)
                for s in range(NT):
                    for k in range(KB):
                        last = mm(t[:, s:s + 1], PB[:, 4 + k, P * s:P * s + P], ones[:, 0:1],
                                  start=(k == 0), stop=(k == KB - 1))
                last.then_inc(s_big_full, 1)
                from_x1("y", 1, 1)
                from_x1("y", 2, 1)
                t = released(("r", 0))
                pe.wait_ge(s_diag_ready, b + 1)
                for half in range(2):
                    cols = slice(HALF * half, HALF * half + HALF)
                    last = mm(t[:, cols], ones[:], PB[:, 0, cols], start=True, stop=True)
                last.then_inc(s_big_full, 1)
                from_x1("y", 3, 1)
                pe.wait_ge(s_ld_u, b * 16 + 16)
                for s in range(NT):
                    t = released(("u", s))
                    split_product(t[:, 0:HALF], lambda h, k: (HH, HL)[h][:, k, P * s:P * s + P],
                                  lambda h, k: w_full[0][:, h, k, :], range(KB)).then_inc(s_big_full, 1)

                def scores1(i):
                    t = released(("s1", i))
                    for half in range(2):
                        cols = slice(HALF * half, HALF * half + HALF)
                        last = split_product(t[:, cols], lambda h, k: ST[:, 4 * h + k, P * i:P * i + P],
                                             lambda h, k: (HH, HL)[h][:, k, cols], range(KB))
                    last.then_inc(s_big_full, 1)

                def values1(c, e, s):
                    use = 4 * c + e
                    if s == 0:
                        if use < 2:
                            pe.wait_ge(s_a_done, b * 16 + 16)
                        else:
                            pe.wait_ge(s_y_out, b * 8 + use - 1 + CREDIT)
                    if e < 2:
                        pe.wait_ge(s_pt_ready, b * 144 + 8 * (UNITS0 + c) + s + 1)
                    ptb = pt_slot(UNITS0 + c, s)
                    for i, (vp, pp) in enumerate(((0, 0), (0, 1), (1, 0))):
                        col = HALF * vp + P * e
                        last = mm(ops[use % 2][:], VT[:, s, col:col + P], ptb[:, pp, :],
                                  start=(s == 0 and i == 0), stop=(s == 7 and i == 2))
                    if s == 7:
                        last.then_inc(s_o_full, 1)

                pe.wait_ge(s_y_ready, b * 4 + 4)
                for i in range(4):
                    scores1(i)
                pe.wait_ge(s_vp_ready, b * 8 + 8)
                for c in range(2):
                    for tb in range(4):
                        if c == 0:
                            scores1(4 + tb)
                        transposes(UNITS0 + c, 2 * tb)
                        transposes(UNITS0 + c, 2 * tb + 1)
                        if tb:
                            for s in (2 * tb - 2, 2 * tb - 1):
                                values1(c, 0, s)
                                values1(c, 1, s)
                    if c == 0 and not last_batch:
                        group_means(2 * b + 3, released(("gna", 1)), mv[:, :, 0], s_gn_mean)
                    for s in (6, 7):
                        values1(c, 0, s)
                        values1(c, 1, s)
                    if c == 1 and not last_batch:
                        group_means(2 * b + 3, released(("gnb", 1)), wvar, s_gn_var)
                    for e in (2, 3):
                        for s in range(8):
                            values1(c, e, s)

            each_batch(pe, body)

        @block.scalar
        def _(act):
            act_fn = nc.scalar.activation

            act.wait_ge(s_in_l1, 13 * 16)
            for j in range(12):
                if j:
                    act.wait_ge(s_square_sum, j)
                act_fn(RB[:, 0:HALF], PB[:, j // 2, HALF * (j % 2):HALF * (j % 2 + 1)], ACT.Square,
                       accum_out=ssq[:, j:j + 1]).then_inc(s_square_sum, 1)
            act.wait_ge(s_in_vout, 16)
            for j in range(4):
                act.wait_ge(s_square_sum, 12 + j)
                act_fn(RB[:, 0:HALF], XA[:, j // 2, HALF * (j % 2):HALF * (j % 2 + 1)], ACT.Square,
                       accum_out=ssq[:, 12 + j:13 + j]).then_inc(s_square_sum, 1)
            act.wait_ge(s_in_l0, 96)
            l0 = [(W[0][:, 0:2048], X[:, 0:2, :]), (W[1][:, 0:2048], X[:, 2:4, :])]
            l0 += [(VT[:, 2 * i, :], XA[:, (2, 3, 0, 1)[i], :]) for i in range(PAIRS)]
            act.wait_ge(s_q_scaled, PAIRS)
            for dst, src in l0:
                act_fn(dst, src if len(src.shape) == 2 else src.rearrange("p a n -> p (a n)"), ACT.Copy)\
                    .then_inc(s_split_hi, 1)
            for i in range(SETUP_BIG):
                act.wait_ge(s_big_full, i + 1)
                dst = (HH[:, :, :], HL[:, :, :], ST[:, 0:4, :])[i // KB].rearrange("p a n -> p (a n)")
                act_fn(dst[:, HALF * (i % KB):HALF * (i % KB) + HALF], big[i % 2][:, 0:HALF], ACT.Copy,
                       scale=SCALE1 if i // KB == 1 else 1.0)\
                    .then_inc(s_prod_hi, 1)

            def norm_hi(n):
                for k in range(KB):
                    act.wait_ge(s_hn_f, n * 4 + k + 1)
                    act_fn(HH[:, k, :], XA[:, k, :], ACT.Copy).then_inc(s_hn_hi, 1)

            act.wait_ge(s_stored_l1, 48)
            norm_hi(0)

            def body(b, last_batch):
                def full(key):
                    i = BIG_AT[key]
                    act.wait_ge(s_big_full, BIG_BASE + b * NBIG + i + 1)
                    return big[i % 2]

                def v_hi(s):
                    t = full(("v", s))
                    act_fn(VT[:, s, :].rearrange("p (q x d) -> p q x d", q=PAIRS, x=4)[:, :, 0:4:3, :],
                           t[:, 0:HALF].rearrange("p (q x d) -> p q x d", q=PAIRS, x=2), ACT.Copy)\
                        .then_inc(s_big_hi, 1)

                def qk_hi(j):
                    t = full(("qk", j))
                    if j >= 2:
                        act.wait_ge(s_stack_a, (b * PAIRS + j // 2) * 96)
                        act.wait_ge(s_stack_b, (b * PAIRS + j // 2) * 96)
                    act_fn(unstacked(j % 2, 0), t[:], ACT.Identity, bias=(bq, bk)[j % 2][:, j // 2:j // 2 + 1])\
                        .then_inc(s_big_hi, 1)

                def exps(u, tb):
                    t = full(("s", 4 * u + tb))
                    act.wait_ge(s_row_max, b * 64 + 4 * u + tb + 1)
                    i = 4 * (u % 2) + tb
                    act_fn(PB[:, i, :], t[:], ACT.Exp, bias=negmax[:, i:i + 1], accum_out=rowsum[:, i:i + 1])\
                        .then_inc(s_exp_done, 1)

                def pt_hi(u, s):
                    n = 8 * u + s
                    act.wait_ge(s_t_full, b * 144 + n + 1)
                    act_fn(pt_slot(u, s)[:, 0, :], tps[n % 2][:], ACT.Copy).then_inc(s_pt_hi, 1)

                def corr(u):
                    act.wait_ge(s_o_full, b * 24 + u + 1 + CREDIT)
                    if u:
                        act.wait_ge(s_a_done, b * 16 + u)
                    lo, to = ((64, 0), (0, 64))[u // 2 % 2]
                    act_fn(RB[to:to + 64, 0:HALF], ops[u % 2][lo:lo + 64, :], ACT.Copy).then_inc(s_corr_done, 1)

                def a_hi(pair):
                    act.wait_ge(s_a_done, b * 16 + 4 * pair + 4)
                    act_fn(HH[:, pair, :], XA[:, pair, :], ACT.Copy).then_inc(s_a_hi, 1)

                for s in range(4):
                    v_hi(s)
                qk_hi(0)
                qk_hi(1)
                for s in range(4, NT):
                    v_hi(s)
                for step in range(STEPS0 + LAG):
                    u, tb, n = step // 4, step % 4, 2 * (step - LAG)
                    if tb == 0 and u % 4 < 2 and u // 4 + 1 < PAIRS:
                        qk_hi(2 * (u // 4 + 1) + u % 4)
                    if n >= 0:
                        pt_hi(n // 8, n % 8)
                        pt_hi(n // 8, n % 8 + 1)
                    if tb == 2 and u >= 2:
                        corr(u - 2)
                    if step < STEPS0:
                        exps(u, tb)
                    if tb == 3 and 13 <= u < 16:
                        a_hi(u - 13)
                corr(UNITS0 - 1)
                a_hi(3)
                for o in range(KB):
                    t = full(("proj", o))
                    if o == 0:
                        act.wait_ge(s_a_lo, b * 4 + 4)
                    act_fn(XA[:, o, :], t[:], ACT.Identity, bias=bp[:, o:o + 1]).then_inc(s_pr_ready, 1)
                for k in range(KB):
                    act.wait_ge(s_res_sum, b * 4 + k + 1)
                    act_fn(X[:, k, :], XA[:, k, :], ACT.Identity, bias=coefB[:, k:k + 1], scale=RES)\
                        .then_inc(s_xc_ready, 1)
                    act.wait_ge(s_xc_ready, b * 4 + k + 1)
                    act_fn(HH[:, k, :], X[:, k, :], ACT.Copy).then_inc(s_xc_hi, 1)
                for k in range(KB):
                    t = full(("y", k))
                    act_fn(ST[:, k, :], t[:], ACT.Copy).then_inc(s_big_hi, 1)
                act.wait_ge(s_diag_ready, b + 1)
                for s in range(NT):
                    t = full(("u", s))
                    act_fn(VT[:, s, 0:HALF], t[:, 0:HALF], ACT.Copy, scale=rcol[:, s:s + 1])\
                        .then_inc(s_big_hi, 1)

                def exps1(i):
                    act.wait_ge(s_neg_ready, b * 8 + i + 1)
                    act_fn(PB[:, i, :], PB[:, i, :], ACT.Exp, bias=negmax[:, i:i + 1], scale=rcol[:, i:i + 1],
                           accum_out=rowsum[:, i:i + 1]).then_inc(s_exp_done, 1)

                for i in range(4):
                    exps1(i)
                for c in range(2):
                    for tb in range(4):
                        pt_hi(UNITS0 + c, 2 * tb)
                        pt_hi(UNITS0 + c, 2 * tb + 1)
                        if c == 0:
                            exps1(4 + tb)
                if not last_batch:
                    norm_hi(b + 1)

            each_batch(act, body)

        @block.gpsimd
        def _(pool):
            nc.gpsimd.memset(ones[:], 1.0)
            nc.gpsimd.memset(expo[:, 0:8], 0.5)
            nc.gpsimd.memset(expo[:, 8:16], -0.5).then_inc(s_const_set, 1)
            pool.wait_ge(s_const_set, 1)
            pool.wait_ge(s_square_sum, 16)
            nc.gpsimd.tensor_tensor(rnorm[:, 0:8], ssq[:, 0:8], expo[:, 8:16], ALU.pow)
            nc.gpsimd.tensor_tensor(rnorm[:, 8:16], ssq[:, 8:16], expo[:, 8:16], ALU.pow).then_inc(s_norm_pow, 1)

            def group_rstd(n):
                pool.wait_ge(s_gn_veps, n)
                nc.gpsimd.tensor_tensor(rstd, veps, expo[:, 8:12], ALU.pow).then_inc(s_gn_rstd, 1)

            group_rstd(1)

            def body(b, last_batch):
                def normalise(n):
                    i = n % 8
                    pool.wait_ge(s_recip_done, b * 72 + n + 1)
                    own_wait(pool)
                    nc.gpsimd.tensor_scalar(PB[:, i, :], PB[:, i, :], rinv[:, i:i + 1], 1.0, ALU.mult, ALU.mult)\
                      .then_inc(s_p_norm, 1)

                def a_lo(pair):
                    pool.wait_ge(s_a_hi, b * 4 + pair + 1)
                    nc.gpsimd.tensor_tensor(HL[:, pair, :], XA[:, pair, :], HH[:, pair, :].bitcast(f32),
                                            ALU.subtract).then_inc(s_a_lo, 1)

                for n in range(4 * UNITS0):
                    normalise(n)
                    if n % 4 == 2 and n // 4 in (14, 15):
                        a_lo(n // 4 - 14)
                a_lo(2)
                a_lo(3)
                group_rstd(2 * b + 2)
                pool.wait_ge(s_ms_done, b + 1)
                nc.gpsimd.tensor_tensor(rms, mean_sq, expo[:, 0:8], ALU.pow).then_inc(s_rms_done, 1)
                for i in range(8):
                    pool.wait_ge(s_s1_ready, b * 8 + i + 1)
                    own_wait(pool)
                    nc.gpsimd.tensor_scalar(negmax[:, i:i + 1], rowmax1[:, i:i + 1], rcol[:, i:i + 1], -1.0,
                                            ALU.mult, ALU.mult).then_inc(s_neg_ready, 1)
                    if i:
                        normalise(64 + i - 1)
                normalise(71)
                if not last_batch:
                    group_rstd(2 * b + 3)

            each_batch(pool, body)

        @block.vector
        def _(dve):
            V = nc.vector

            links = [0, 0]

            def link(instruction):
                instruction.then_inc(s_dve_step, 1)
                links[1] += 1
                dve.wait_ge(s_dve_step, links[0] + links[1])

            dve.sem_inc(s_y_out, CREDIT)
            dve.wait_ge(s_in_vec, 48)
            dve.wait_ge(s_norm_pow, 1)
            link(V.tensor_tensor(wscale, rnorm, g_l1, ALU.mult))
            link(V.tensor_scalar(wscale[:, 12:16], wscale[:, 12:16], RES, None, ALU.mult))
            for j in range(12):
                blk = PB[:, j // 2, HALF * (j % 2):HALF * (j % 2 + 1)]
                V.tensor_scalar(blk, blk, wscale[:, j:j + 1], None, ALU.mult).then_inc(s_w_normed, 1)
            link(V.tensor_scalar(bq, bq, SCALE0, None, ALU.mult))
            dve.wait_ge(s_in_l0, 96)
            for i in range(PAIRS):
                wq = XA[:, i, :].rearrange("p (k n) -> p k n", k=KB)[:, :, 0:P]
                V.tensor_scalar(wq, wq, SCALE0, None, ALU.mult).then_inc(s_q_scaled, 1)
            l0 = [(W[0], X[:, 0:2, :]), (W[1], X[:, 2:4, :])]
            for i, (w, src) in enumerate(l0):
                dve.wait_ge(s_split_hi, i + 1)
                V.tensor_tensor(w[:, 2048:4096], src.rearrange("p a n -> p (a n)"), w[:, 0:2048].bitcast(f32),
                                ALU.subtract).then_inc(s_split_lo, 1)
            for i in range(PAIRS):
                dve.wait_ge(s_split_hi, i + 3)
                V.tensor_tensor(VT[:, 2 * i + 1, :], XA[:, (2, 3, 0, 1)[i], :], VT[:, 2 * i, :].bitcast(f32),
                                ALU.subtract).then_inc(s_split_lo, 1)
            for i in range(SETUP_BIG):
                dve.wait_ge(s_prod_hi, i + 1)
                dst = (HH[:, :, :], HL[:, :, :], ST[:, 0:4, :])[i // KB].rearrange("p a n -> p (a n)")
                hi = dst[:, HALF * (i % KB):HALF * (i % KB) + HALF]
                V.scalar_tensor_tensor(dst[:, 2048 + HALF * (i % KB):2048 + HALF * (i % KB) + HALF],
                                       big[i % 2][:, 0:HALF], SCALE1 if i // KB == 1 else 1.0, hi.bitcast(f32),
                                       ALU.mult, ALU.subtract).then_inc(s_prod_lo, 1)

            def channel_stats(k):
                V.bn_stats(stats[:, k, 0:6], XA[:, k, 0:HALF])
                link(V.bn_stats(stats[:, k, 6:12], XA[:, k, HALF:N]))
                own_wait(dve)
                return V.bn_aggr(mv[:, k, :], stats[:, k, :])

            def group_var(tile, full_at):
                dve.wait_ge(s_big_full, full_at)
                link(V.tensor_copy(gmean, tile[:, 0:KB]))
                link(V.tensor_tensor(dev, mv[:, :, 0], gmean, ALU.subtract))
                link(V.tensor_tensor(dev, dev, dev, ALU.mult))
                V.tensor_tensor(wvar, dev, mv[:, :, 1], ALU.add).then_inc(s_gn_var, 1)

            def group_coefs(n, tile, full_at, scale, bias, times):
                dve.wait_ge(s_big_full, full_at)
                V.tensor_scalar(veps, tile[:, 0:KB], GN_EPS, None, ALU.add).then_inc(s_gn_veps, 1)
                dve.wait_ge(s_gn_rstd, n)
                link(V.tensor_tensor(coefA, rstd, scale, ALU.mult))
                link(V.tensor_tensor(coefT, gmean, coefA, ALU.mult))
                link(V.tensor_tensor(coefB, bias, coefT, ALU.subtract))
                if times != 1.0:
                    link(V.tensor_scalar(coefB, coefB, times, None, ALU.mult))

            def norm_split(n):
                for k in range(KB):
                    V.tensor_scalar(XA[:, k, :], XA[:, k, :], coefA[:, k:k + 1], coefB[:, k:k + 1],
                                    ALU.mult, ALU.add).then_inc(s_hn_f, 1)
                for k in range(KB):
                    dve.wait_ge(s_hn_hi, n * 4 + k + 1)
                    V.tensor_tensor(HL[:, k, :], XA[:, k, :], HH[:, k, :].bitcast(f32), ALU.subtract)\
                     .then_inc(s_hn_ready, 1)

            dve.wait_ge(s_x_next, 16)
            for k in range(KB):
                last = channel_stats(k)
            last.then_inc(s_gn_mean, 1)
            dve.wait_ge(s_gn_mean, 1)
            group_var(big[0], SETUP_BIG + 1)
            group_coefs(1, big[1], SETUP_BIG + 2, gs1, gb1, 1.0)
            dve.wait_ge(s_stored_l1, 48)
            norm_split(0)
            dve.wait_ge(s_stored_l0, 96)
            links_before = links[1]

            def body(b, last_batch):
                links[0], links[1] = links_before + b * DVE_LINKS, 0

                def at(key):
                    return big_count(b, key)

                def tile(key):
                    return big[BIG_AT[key] % 2]

                def v_lo(s):
                    dve.wait_ge(s_big_hi, hi_count(b, ("v", s)))
                    v = VT[:, s, :].rearrange("p (q x d) -> p q x d", q=PAIRS, x=4)
                    V.tensor_tensor(v[:, :, 1:3, :], tile(("v", s))[:, 0:HALF].rearrange("p (q x d) -> p q x d", q=PAIRS, x=2),
                                    v[:, :, 0:4:3, :].bitcast(f32), ALU.subtract).then_inc(s_v_ready, 1)

                def qk_lo(j):
                    dve.wait_ge(s_big_hi, hi_count(b, ("qk", j)))
                    V.scalar_tensor_tensor(unstacked(j % 2, 1), tile(("qk", j))[:], (bq, bk)[j % 2][:, j // 2:j // 2 + 1],
                                           unstacked(j % 2, 0).bitcast(f32), ALU.add, ALU.subtract)\
                     .then_inc(s_nat_ready, 1)

                def row_max(u, tb):
                    i = 4 * (u % 2) + tb
                    dve.wait_ge(s_big_full, at(("s", 4 * u + tb)))
                    V.tensor_reduce(negmax[:, i:i + 1], tile(("s", 4 * u + tb))[:], axis=AX.X, op=ALU.max,
                                    negate=True).then_inc(s_row_max, 1)

                def recip(u, tb):
                    i = 4 * (u % 2) + tb
                    dve.wait_ge(s_exp_done, b * 72 + 4 * u + tb + 1)
                    V.reciprocal(rinv[:, i:i + 1], rowsum[:, i:i + 1]).then_inc(s_recip_done, 1)

                def pt_lo(u, s):
                    n = 8 * u + s
                    dve.wait_ge(s_pt_hi, b * 144 + n + 1)
                    V.tensor_tensor(pt_slot(u, s)[:, 1, :], tps[n % 2][:], pt_slot(u, s)[:, 0, :].bitcast(f32),
                                    ALU.subtract).then_inc(s_pt_ready, 1)

                def head_out(u):
                    dve.wait_ge(s_corr_done, b * 16 + u + 1)
                    r = slice(64 * (u // 2 % 2), 64 * (u // 2 % 2) + 64)
                    pair, c = u // 4, u % 2
                    V.scalar_tensor_tensor(XA[r, pair, HALF * c:HALF * c + HALF], ops[u % 2][r, :], bv[r, pair:pair + 1],
                                           RB[r, 0:HALF], ALU.add, ALU.add).then_inc(s_a_done, 1)

                for s in range(4):
                    v_lo(s)
                qk_lo(0)
                qk_lo(1)
                for s in range(4, NT):
                    v_lo(s)
                for step in range(STEPS0 + LAG):
                    u, tb, n = step // 4, step % 4, 2 * (step - LAG)
                    if tb == 0 and u % 4 < 2 and u // 4 + 1 < PAIRS:
                        qk_lo(2 * (u // 4 + 1) + u % 4)
                    if 1 <= step <= STEPS0:
                        recip((step - 1) // 4, (step - 1) % 4)
                    if step < STEPS0:
                        row_max(u, tb)
                    if n >= 0:
                        pt_lo(n // 8, n % 8)
                        pt_lo(n // 8, n % 8 + 1)
                    if tb == 2 and u >= 2:
                        head_out(u - 2)
                head_out(UNITS0 - 1)

                for k in range(KB):
                    dve.wait_ge(s_pr_ready, b * 4 + k + 1)
                    last = channel_stats(k)
                last.then_inc(s_gn_mean, 1)
                dve.wait_ge(s_gn_mean, 2 * b + 2)
                group_var(tile(("gna", 0)), at(("gna", 0)))
                group_coefs(2 * b + 2, tile(("gnb", 0)), at(("gnb", 0)), gs2, gb2, RES)
                dve.wait_ge(s_x_res, b * 16 + 16)
                for k in range(KB):
                    V.scalar_tensor_tensor(XA[:, k, :], XA[:, k, :], coefA[:, k:k + 1], X[:, k, :], ALU.mult, ALU.add)\
                     .then_inc(s_res_sum, 1)
                    if k:
                        xc_lo(b, k - 1)
                xc_lo(b, KB - 1)

                for k in range(KB):
                    dve.wait_ge(s_big_full, at(("g", k)))
                    V.tensor_tensor(PB[:, 4 + k, :], tile(("g", k))[:], X[:, k, :], ALU.mult)\
                     .then_inc(s_prod_ready, 1)

                def y_lo(k):
                    dve.wait_ge(s_big_hi, hi_count(b, ("y", k)))
                    V.tensor_tensor(ST[:, 4 + k, :], tile(("y", k))[:], ST[:, k, :].bitcast(f32), ALU.subtract)\
                     .then_inc(s_y_ready, 1)

                y_lo(0)
                dve.wait_ge(s_big_full, at(("sum", 0)))
                V.tensor_scalar(mean_sq, tile(("sum", 0))[:, 0:8], 1.0 / (3 * C * RES * RES), 0.0, ALU.mult, ALU.max)\
                 .then_inc(s_ms_done, 1)
                dve.wait_ge(s_rms_done, b + 1)
                link(V.tensor_scalar(rms, rms, RMS_EPS, RES, ALU.add, ALU.mult))
                link(V.reciprocal(rcol, rms))
                for s in range(NT):
                    last = V.tensor_scalar(PB[:, 0, P * s:P * s + P], ident[:], rcol[:, s:s + 1], None, ALU.mult)
                last.then_inc(s_diag_ready, 1)
                y_lo(1)
                y_lo(2)
                dve.wait_ge(s_big_full, at(("r", 0)))
                V.tensor_copy(RB[:], tile(("r", 0))[:]).then_inc(s_r_ready, 1)
                y_lo(3)
                for s in range(NT):
                    dve.wait_ge(s_big_hi, hi_count(b, ("u", s)))
                    V.scalar_tensor_tensor(VT[:, s, HALF:N], tile(("u", s))[:, 0:HALF], rcol[:, s:s + 1],
                                           VT[:, s, 0:HALF].bitcast(f32), ALU.mult, ALU.subtract)\
                     .then_inc(s_vp_ready, 1)

                def scaled_max(i):
                    dve.wait_ge(s_big_full, at(("s1", i)))
                    if i == 0:
                        dve.wait_ge(s_r_ready, b + 1)
                    own_wait(dve)
                    V.tensor_tensor_reduce(out=PB[:, i, :], in0=tile(("s1", i))[:], in1=RB[:], scale=1.0,
                                           scalar=NEG, op0=ALU.mult, op1=ALU.max,
                                           accum_out=rowmax1[:, i:i + 1]).then_inc(s_s1_ready, 1)

                def recip1(i):
                    dve.wait_ge(s_exp_done, b * 72 + 64 + i + 1)
                    V.reciprocal(rinv[:, i:i + 1], rowsum[:, i:i + 1]).then_inc(s_recip_done, 1)

                def layer_out(j):
                    c, e = j // 4, j % 4
                    dve.wait_ge(s_o_full, b * 24 + UNITS0 + j + 1 + CREDIT)
                    xs = X[:, e, HALF * c:HALF * c + HALF]
                    V.scalar_tensor_tensor(xs, ops[j % 2][:], wscale[:, 12 + e:13 + e], xs, ALU.mult, ALU.add)\
                     .then_inc(s_y_out, 1)

                for i in range(4):
                    scaled_max(i)
                    if i:
                        recip1(i - 1)
                recip1(3)
                for tb in range(4):
                    scaled_max(4 + tb)
                    if not last_batch:
                        if tb == 0:
                            dve.wait_ge(s_x_next, (b + 2) * 16)
                        last = channel_stats(tb)
                        if tb == 3:
                            last.then_inc(s_gn_mean, 1)
                    pt_lo(UNITS0, 2 * tb)
                    pt_lo(UNITS0, 2 * tb + 1)
                    recip1(4 + tb)
                if not last_batch:
                    dve.wait_ge(s_gn_mean, 2 * b + 3)
                    group_var(tile(("gna", 1)), at(("gna", 1)))
                for j in range(4):
                    layer_out(j)
                for s in range(NT):
                    pt_lo(UNITS0 + 1, s)
                if not last_batch:
                    group_coefs(2 * b + 3, tile(("gnb", 1)), at(("gnb", 1)), gs1, gb1, 1.0)
                layer_out(4)
                layer_out(5)
                if not last_batch:
                    norm_split(b + 1)
                layer_out(6)
                layer_out(7)
                if not last_batch:
                    assert links[1] == DVE_LINKS, links[1]

            def xc_lo(b, k):
                dve.wait_ge(s_xc_hi, b * 4 + k + 1)
                V.tensor_tensor(HL[:, k, :], X[:, k, :], HH[:, k, :].bitcast(f32), ALU.subtract)\
                 .then_inc(s_xc_lo, 1)

            each_batch(dve, body)


NEG = -3.0e38


def kernel(**inputs):
    import numpy as np
    import concourse.bacc as bacc
    from concourse.bass_utils import run_bass_kernel_spmd

    nc = bacc.Bacc("TRN2", target_bir_lowering=False, num_devices=1, dynamic_dma_scratch_size=1024)
    g = {k: np.asarray(v) for k, v in inputs.items()}

    def blocks(w_t, cols):
        return np.ascontiguousarray(w_t.reshape(KB, P, cols).transpose(1, 0, 2).reshape(P, KB * cols))

    def columns(v):
        return v.reshape(-1, P).T

    w = g["L0_conv_w_qkv"].reshape(HEADS, 3, CH, C)
    bqkv = g["L0_conv_b_qkv"].reshape(HEADS, 3, CH)
    wqk = [blocks(np.concatenate([w[2 * p:2 * p + 2, j].reshape(P, C) for j in (0, 1)]).T, 2 * P) for p in range(PAIRS)]
    arrays = {
        "x": g["x"].reshape(B, C, N),
        "wv_t": blocks(w[:, 2].reshape(C, C).T, C),
        "wp_t": blocks(g["L0_conv_w_proj"].T, C),
        "wqk_t": np.stack(wqk),
        "v_qkv": g["L1_conv_v_qkv"].reshape(12, P, C),
        "v_out": blocks(g["L1_conv_v_out"], C),
        "wo_t": blocks(g["L1_conv_v_out"].T, C),
        "vecs": np.concatenate([columns(bqkv[:, j].reshape(C)) for j in range(3)]
                               + [columns(g[k]) for k in ("L0_conv_gn1_scale", "L0_conv_gn1_bias", "L0_conv_gn2_scale",
                                                          "L0_conv_gn2_bias", "L0_conv_b_proj", "L1_conv_g_qkv",
                                                          "L1_conv_g_out")], axis=1),
        "consts": np.stack([np.eye(P, dtype=np.float32),
                            np.kron(np.eye(P // 16), np.full((16, 16), 1 / 16)).astype(np.float32)]),
    }
    arrays = {f"in_{k}": np.ascontiguousarray(v) for k, v in arrays.items()}
    aps = [nc.dram_tensor(k, v.shape, f32, kind="ExternalInput").ap() for k, v in arrays.items()]
    out = nc.dram_tensor("out", (B, C, N), f32, kind="ExternalOutput").ap()
    build(nc, *aps, out)
    r = run_bass_kernel_spmd(nc, [arrays], core_ids=[0])
    return r.results[0]["out"].reshape(B, C, 32, 32)
```

```python
import concourse.bass as bass
from concourse import mybir
from contextlib import ExitStack

B, C, N = 8, 512, 1024
HEADS = 8
CH = C // HEADS
P = 128
KB = C // P
NT = N // P
HALF = 512
PAIRS = HEADS // 2
UNITS0 = HEADS * 2
UNITS = UNITS0 + 2
STEPS0 = 4 * UNITS0
GN_EPS = 1e-5
RMS_EPS = 1e-4
RES = 2.0 ** -0.5

f32 = mybir.dt.float32
f32r = mybir.dt.float32r
ACT = mybir.ActivationFunctionType
ALU = mybir.AluOpType
AX = mybir.AxisListType

QK_STEPS = (5, 7, 9, 11)


def qk_part(step):
    if step % 16 in QK_STEPS and step < STEPS0 - 16:
        return 4 * (step // 16 + 1) + QK_STEPS.index(step % 16)
    return None


def a_parts(step):
    return [divmod(i, 2) for i, at in enumerate(A_STEPS) if at == step]


A_STEPS = (47, 49, 51, 53, 57, 60)
BIG = [("v", 0)] + [("qk", j) for j in range(4)] + [("v", 1), ("v", 2), ("v", 3)]
for _step in range(STEPS0):
    if qk_part(_step) is not None:
        BIG.append(("qk", qk_part(_step)))
    BIG.append(("s", _step))
BIG += [("proj", k) for k in range(KB)] + [("gna", 0), ("gnb", 0)] + [("g", k) for k in range(KB)]
BIG += [("y", 0), ("y", 1), ("sum", 0), ("y", 2), ("y", 3), ("u", 0), ("u", 1), ("u", 2), ("r", 0)]
BIG += [("u", s) for s in range(3, NT)] + [("s1", t) for t in range(5)]
BIG += [("gna", 1), ("s1", 5), ("gnb", 1), ("s1", 6), ("s1", 7)]
NBIG = len(BIG)
assert NBIG % 2 == 0
HI = [key for key in BIG if key[0] in ("v", "qk", "y", "u")]
BIG_LAST = [key for key in BIG if key not in (("gna", 1), ("gnb", 1))]
SETUP_BIG = 3 * KB
BIG_BASE = SETUP_BIG + 2
DVE_LINKS = 24
SCALE0 = float(CH) ** -0.5
SCALE1 = float(C) ** -0.5
XC_PARTS = [(0, slice(0, HALF)), (0, slice(HALF, N))] + [(k, slice(0, N)) for k in range(1, KB)]
LAG = 5
CREDIT = 1


def build(nc, x, wv_t, wp_t, wqk_t, v_qkv, v_out, wo_t, vecs, consts, out):
    ctx = ExitStack()
    with ctx:
        def sb(name, shape, dt=f32):
            return ctx.enter_context(nc.sbuf_tensor(name, shape, dt))

        def ps(name, cols):
            return ctx.enter_context(nc.psum_tensor(name, [P, cols], f32))

        def sem(name):
            return ctx.enter_context(nc.semaphore(name))

        d_wv = nc.dram_tensor("d_wv", [P, 4096], f32)
        d_wp = nc.dram_tensor("d_wp", [P, 4096], f32)
        d_qk = nc.dram_tensor("d_qk", [PAIRS, P, 2048], f32)
        d_g = nc.dram_tensor("d_g", [P, 4096], f32)
        d_m = nc.dram_tensor("d_m", [P, 4096], f32)
        d_u = nc.dram_tensor("d_u", [P, 4096], f32)

        X = sb("X", [P, KB, N])
        XA = sb("XA", [P, KB, N])
        HH = sb("HH", [P, KB, N], f32r)
        HL = sb("HL", [P, KB, N], f32r)
        VT = sb("VT", [P, NT, N], f32r)
        ST = sb("ST", [P, 10, N], f32r)
        PB = sb("PB", [P, 8, N])
        PT = sb("PT", [P, 4, 2, HALF], f32r)
        W = [sb("W0", [P, 4096], f32r), sb("W1", [P, 4096], f32r)]
        RB = sb("RB", [P, N])
        ident = sb("ident", [P, P])
        gavg = sb("gavg", [P, P])
        ones = sb("ones", [P, P])
        vec = sb("vec", [P, 48])
        small = sb("small", [P, 208])
        stats = small[:, 0:48].rearrange("p (k s) -> p k s", k=KB)
        mv = small[:, 48:56].rearrange("p (k s) -> p k s", k=KB)
        gmean, dev, wvar = small[:, 56:60], small[:, 60:64], small[:, 64:68]
        veps, rstd, coefA = small[:, 68:72], small[:, 72:76], small[:, 76:80]
        coefT, coefB = small[:, 80:84], small[:, 84:88]
        negmax, rowsum, rinv = small[:, 88:96], small[:, 96:104], small[:, 104:112]
        mean_sq, rms, rcol = small[:, 112:120], small[:, 120:128], small[:, 128:136]
        rowmax1 = small[:, 136:144]
        ssq, rnorm, wscale = small[:, 144:160], small[:, 160:176], small[:, 176:192]
        expo = small[:, 192:208]
        bq, bk, bv = vec[:, 0:4], vec[:, 4:8], vec[:, 8:12]
        gs1, gb1, gs2, gb2, bp = (vec[:, 12 + 4 * i:16 + 4 * i] for i in range(5))
        g_l1 = vec[:, 32:48]

        big = [ps("big0", N), ps("big1", N)]
        tps = [ps("tps0", HALF), ps("tps1", HALF)]
        ops = [ps("ops0", HALF), ps("ops1", HALF)]

        PT1 = W[1][:, 2048:4096].rearrange("p (s h n) -> p s h n", s=2, h=2)

        def pt_slot(u, s):
            if u < UNITS0:
                return PT[:, s % 4, :, :]
            if s < 4:
                return PT[:, s, :, :]
            return ST[:, s + 4, :].rearrange("p (h n) -> p h n", h=2) if s < 6 else PT1[:, s - 6, :, :]

        def v_heads(i):
            return VT[:, 2 * i:2 * i + 2, :].rearrange("p t n -> p (t n)").rearrange("p (q x d) -> p q x d", x=4, d=CH)

        def stack(kind, head):
            return ST[:, {"q": 0, "kh": 2, "kl": 4}[kind] + head, :]

        def unstacked(kind, part):
            return ST[:, 6 + 2 * kind + part, :]

        w_full = [w[:, :].rearrange("p (h k n) -> p h k n", h=2, k=KB) for w in W]

        def w_qk(pair):
            w = W[1 if pair < 2 else 0][:, 2048 * (pair % 2):2048 * (pair % 2) + 2048]
            return w.rearrange("p (h k n) -> p h k n", h=2, k=KB)

        s_waited = sem("waited")
        s_q_scaled = sem("q_scaled")
        s_in_l0 = sem("in_l0")
        s_in_l1v = sem("s_in_l1v")
        s_in_l1 = sem("in_l1")
        s_in_vout = sem("in_vout")
        s_in_vec = sem("in_vec")
        s_split_hi = sem("split_hi")
        s_split_lo = sem("split_lo")
        s_stored_l0 = sem("stored_l0")
        s_square_sum = sem("square_sum")
        s_norm_pow = sem("norm_pow")
        s_w_normed = sem("w_normed")
        s_prod_hi = sem("prod_hi")
        s_prod_lo = sem("prod_lo")
        s_stored_l1 = sem("stored_l1")
        s_dve_step = sem("dve_step")
        s_expo_set = sem("s_expo_set")
        s_const_set = sem("const_set")
        s_x_next = sem("x_next")
        s_x_res = sem("x_res")
        s_ld_wv = sem("ld_wv")
        s_ld_wp = sem("ld_wp")
        s_ld_g = sem("ld_g")
        s_ld_m = sem("ld_m")
        s_ld_u = sem("ld_u")
        s_stack_a = sem("stack_a")
        s_stack_b = sem("stack_b")
        s_out_done = sem("out_done")
        s_big_full = sem("big_full")
        s_big_hi = sem("big_hi")
        s_v_ready = sem("v_ready")
        s_nat_ready = sem("nat_ready")
        s_t_full = sem("t_full")
        s_pt_hi = sem("pt_hi")
        s_pt_ready = sem("pt_ready")
        s_o_full = sem("o_full")
        s_row_max = sem("row_max")
        s_exp_done = sem("exp_done")
        s_recip_done = sem("recip_done")
        s_p_norm = sem("p_norm")
        s_corr_done = sem("corr_done")
        s_a_done = sem("a_done")
        s_a_hi = sem("a_hi")
        s_a_lo = sem("a_lo")
        s_a_lo_last = sem("s_a_lo_last")
        s_pr_ready = sem("pr_ready")
        s_gn_mean = sem("gn_mean")
        s_gn_var = sem("gn_var")
        s_gn_veps = sem("gn_veps")
        s_gn_rstd = sem("gn_rstd")
        s_coef_b = sem("coef_b")
        s_res_sum = sem("res_sum")
        s_xc_ready = sem("xc_ready")
        s_xc_hi = sem("xc_hi")
        s_xc_lo = sem("xc_lo")
        s_prod_ready = sem("prod_ready")
        s_prod_sum = sem("prod_sum")
        s_ms_done = sem("ms_done")
        s_rms_done = sem("rms_done")
        s_diag_ready = sem("diag_ready")
        s_r_ready = sem("r_ready")
        s_y_ready = sem("y_ready")
        s_vp_ready = sem("vp_ready")
        s_s1_ready = sem("s1_ready")
        s_neg_ready = sem("neg_ready")
        s_hn_f = sem("hn_f")
        s_hn_hi = sem("hn_hi")
        s_hn_ready = sem("hn_ready")
        s_y_out = sem("y_out")
        ld_qk = [sem(f"ld_qk{i}") for i in range(PAIRS)]
        block = ctx.enter_context(nc.Block())

        def each_batch(eng, body):
            with eng.Fori(0, B - 1) as b:
                body(b, False)
            body(B - 1, True)

        def w1_block(j, start=0, stop=HALF):
            return PB[:, j // 2, HALF * (j % 2) + start:HALF * (j % 2) + stop]

        def product_stage(i):
            return (ST[:, 4:8, :].rearrange("p a n -> p (a n)"), PT[:, :, :, :].rearrange("p a h n -> p (a h n)"),
                    ST[:, 0:4, :].rearrange("p a n -> p (a n)"))[i]

        def product_parts(i):
            k = i % KB
            if i // KB == 0:
                return [(slice(0, HALF), 1.0)]
            if i // KB == 1:
                return [(slice(0, HALF), SCALE1)]
            return [(slice(P * k, P * k + P), 1.0)] + ([(slice(P * k + P, HALF), 2.0)] if k < KB - 1 else [])

        def big_at(b, key):
            return (BIG_LAST if isinstance(b, int) else BIG).index(key)

        def big_count(b, key):
            return BIG_BASE + b * NBIG + big_at(b, key) + 1

        def hi_count(b, key):
            return b * len(HI) + HI.index(key) + 1

        def own_wait(eng):
            eng.sem_inc(s_waited, 1)

        def src_x(b):
            return x[b].rearrange("(k p) n -> p k n", p=P)

        @block.sync
        def _(sp):
            sp.sem_inc(s_out_done, 16 * CREDIT)
            sp.dma_start(vec[:], vecs).then_inc(s_in_vec, 16)
            sp.dma_start(ident[:], consts[0]).then_inc(s_in_vec, 16)
            sp.dma_start(gavg[:], consts[1]).then_inc(s_in_vec, 16)
            for j in (8, 9, 10, 11):
                sp.dma_start(w1_block(j), v_qkv[j]).then_inc(s_in_l1v, 16)
            sp.dma_start(PB[:, 6:8, :].rearrange("p a n -> p (a n)"), wo_t).then_inc(s_in_l1v, 16)
            for j in range(8):
                sp.dma_start(w1_block(j), v_qkv[j]).then_inc(s_in_l1, 16)
            sp.dma_start(XA[:, 0:2, :].rearrange("p a n -> p (a n)"), v_out).then_inc(s_in_vout, 16)
            sp.dma_start(X[:, 0:2, :].rearrange("p a n -> p (a n)"), wv_t).then_inc(s_in_l0, 16)
            sp.dma_start(X[:, 2:4, :].rearrange("p a n -> p (a n)"), wp_t).then_inc(s_in_l0, 16)
            for i in range(2):
                sp.dma_start(XA[:, 2 + i, :], wqk_t[i]).then_inc(s_in_l0, 16)
            sp.wait_ge(s_square_sum, 16)
            for i in range(2):
                sp.dma_start(XA[:, i, :], wqk_t[2 + i]).then_inc(s_in_l0, 16)
            sp.wait_ge(s_split_lo, 6)
            sp.dma_start(d_wv[:], W[0][:].bitcast(f32)).then_inc(s_stored_l0, 16)
            sp.dma_start(d_wp[:], W[1][:].bitcast(f32)).then_inc(s_stored_l0, 16)
            for i in range(PAIRS):
                sp.dma_start(d_qk[i], VT[:, 2 * i:2 * i + 2, :].rearrange("p a n -> p (a n)").bitcast(f32))\
                  .then_inc(s_stored_l0, 16)
            sp.dma_start(XA[:], src_x(0)).then_inc(s_x_next, 16)
            for i, dst in enumerate((d_u, d_m, d_g)):
                sp.wait_ge(s_prod_lo, KB * (i + 1))
                sp.dma_start(dst[:], product_stage(i).bitcast(f32)).then_inc(s_stored_l1, 16)
            sp.wait_ge(s_stored_l0, 96)
            sp.wait_ge(s_stored_l1, 48)
            sp.dma_start(W[0][:].bitcast(f32), d_wv[:]).then_inc(s_ld_wv, 16)
            sp.dma_start(w_qk(0).rearrange("p h k n -> p (h k n)").bitcast(f32), d_qk[0]).then_inc(ld_qk[0], 16)

            def stack_head(b, pair, head):
                rows = slice(64 * head, 64 * head + 64)
                s_stack = (s_stack_a, s_stack_b)[head]
                sp.wait_ge(s_nat_ready, b * 16 + 4 * pair + 4)
                own_wait(sp)
                if pair:
                    sp.wait_ge(s_big_full, big_count(b, ("s", 16 * (pair - 1) + 8 * head + 7)))
                    own_wait(sp)
                moves = [("q", 64 * head, 0, 0), ("q", 64 - 64 * head, 0, 1)]
                moves += [("kh", q, 1, 0) for q in (0, 64)] + [("kl", q, 1, 1) for q in (0, 64)]
                for kind, to, what, part in moves:
                    sp.dma_start(stack(kind, head)[to:to + 64, :].bitcast(f32),
                                 unstacked(what, part)[rows, :].bitcast(f32))\
                      .then_inc(s_stack, 16)

            def body(b, last):
                sp.wait_ge(s_o_full, b * 24 + CREDIT)
                own_wait(sp)
                sp.dma_start(w_qk(1).rearrange("p h k n -> p (h k n)").bitcast(f32), d_qk[1]).then_inc(ld_qk[1], 16)
                stack_head(b, 0, 0)
                stack_head(b, 0, 1)
                sp.wait_ge(s_out_done, (b * 8 + CREDIT) * 16)
                own_wait(sp)
                sp.dma_start(X[:], src_x(b)).then_inc(s_x_res, 16)
                sp.wait_ge(s_big_full, big_count(b, ("v", NT // 2 - 1)))
                own_wait(sp)
                for i in (2, 3):
                    sp.dma_start(w_qk(i).rearrange("p h k n -> p (h k n)").bitcast(f32), d_qk[i]).then_inc(ld_qk[i], 16)
                stack_head(b, 1, 0)
                sp.dma_start(W[1][:].bitcast(f32), d_wp[:]).then_inc(s_ld_wp, 16)
                stack_head(b, 1, 1)
                stack_head(b, 2, 0)
                stack_head(b, 2, 1)
                stack_head(b, 3, 0)
                sp.dma_start(W[0][:].bitcast(f32), d_g[:]).then_inc(s_ld_g, 16)
                stack_head(b, 3, 1)
                sp.wait_ge(s_big_full, big_count(b, ("proj", KB - 1)))
                own_wait(sp)
                sp.dma_start(W[1][:].bitcast(f32), d_m[:]).then_inc(s_ld_m, 16)
                if not last:
                    sp.wait_ge(s_xc_ready, (b + 1) * len(XC_PARTS))
                    sp.wait_ge(s_xc_hi, (b + 1) * len(XC_PARTS))
                    own_wait(sp)
                    sp.dma_start(XA[:], src_x(b + 1)).then_inc(s_x_next, 16)
                sp.wait_ge(s_big_full, big_count(b, ("g", KB - 1)))
                own_wait(sp)
                sp.dma_start(W[0][:].bitcast(f32), d_u[:]).then_inc(s_ld_u, 16)
                if not last:
                    sp.wait_ge(s_big_full, big_count(b, ("y", KB - 1)))
                    own_wait(sp)
                    sp.dma_start(w_qk(0).rearrange("p h k n -> p (h k n)").bitcast(f32), d_qk[0])\
                      .then_inc(ld_qk[0], 16)
                    sp.wait_ge(s_big_full, big_count(b, ("u", NT - 1)))
                    own_wait(sp)
                    sp.dma_start(W[0][:].bitcast(f32), d_wv[:]).then_inc(s_ld_wv, 16)
                for j in range(8):
                    sp.wait_ge(s_y_out, b * 8 + j + 1 + CREDIT)
                    own_wait(sp)
                    c, e = j // 4, j % 4
                    sp.dma_start(out[b].rearrange("(k p) n -> p k n", p=P)[:, e, HALF * c:HALF * c + HALF],
                                 X[:, e, HALF * c:HALF * c + HALF]).then_inc(s_out_done, 16)

            each_batch(sp, body)
            sp.wait_ge(s_out_done, (B * 8 + CREDIT) * 16)

        @block.tensor
        def _(pe):
            mm = nc.tensor.matmul

            def split_product(dst, stat, mov, ks):
                n, i = 3 * len(ks), 0
                for k in ks:
                    for sp_, mp_ in ((0, 0), (0, 1), (1, 0)):
                        last = mm(dst, stat(sp_, k), mov(mp_, k), start=(i == 0), stop=(i == n - 1))
                        i += 1
                return last

            def group_means(n, tile, operand, ready):
                pe.wait_ge(ready, n)
                mm(tile[:, 0:KB], gavg[:], operand, start=True, stop=True).then_inc(s_big_full, 1)

            pe.sem_inc(s_o_full, CREDIT)
            pe.wait_ge(s_in_l1v, 5 * 16)
            pe.wait_ge(s_w_normed, 4)
            for i in range(KB):
                if i >= 2:
                    pe.wait_ge(s_prod_lo, i - 1)
                for j in range(4):
                    last = mm(big[i % 2][:, 0:HALF], w1_block(8 + j, P * i, P * i + P),
                              PB[:, 6 + j // 2, HALF * (j % 2):HALF * (j % 2 + 1)], start=(j == 0), stop=(j == 3))
                last.then_inc(s_big_full, 1)
            pe.wait_ge(s_w_normed, 12)
            for i in range(KB):
                pe.wait_ge(s_prod_lo, KB + i - 1)
                for j in range(4):
                    last = mm(big[i % 2][:, 0:HALF], w1_block(j, P * i, P * i + P), w1_block(4 + j),
                              start=(j == 0), stop=(j == 3))
                last.then_inc(s_big_full, 1)
            for i in range(KB):
                pe.wait_ge(s_prod_lo, 2 * KB + i - 1)
                for j in range(12):
                    last = mm(big[i % 2][:, P * i:HALF], w1_block(j, P * i, P * i + P), w1_block(j, P * i),
                              start=(j == 0), stop=(j == 11))
                last.then_inc(s_big_full, 1)
            pe.wait_ge(s_in_vec, 48)
            pe.wait_ge(s_prod_lo, SETUP_BIG - 1)
            group_means(1, big[0], mv[:, :, 0], s_gn_mean)
            pe.wait_ge(s_prod_lo, SETUP_BIG)
            group_means(1, big[1], wvar, s_gn_var)
            pe.wait_ge(s_const_set, 1)

            def body(b, last_batch):
                def released(key):
                    i = big_at(b, key)
                    if i >= 2:
                        kind, k = (BIG_LAST if last_batch else BIG)[i - 2]
                        reader, per = {"v": (s_v_ready, 4), "qk": (s_nat_ready, 16), "s": (s_exp_done, 72),
                                       "proj": (s_pr_ready, 4), "gna": (s_gn_var, 2), "gnb": (s_gn_veps, 2),
                                       "g": (s_prod_ready, 4), "sum": (s_ms_done, 1), "r": (s_r_ready, 1),
                                       "y": (s_y_ready, 4), "u": (s_vp_ready, 8), "s1": (s_s1_ready, 8)}[kind]
                        pe.wait_ge(reader, b * per + k + (2 if kind in ("gna", "gnb") else 1))
                    else:
                        pe.wait_ge(s_gn_veps, 2 * b + 1)
                    return big[i % 2]

                pe.wait_ge(s_hn_ready, b * KB + KB)
                pe.wait_ge(s_ld_wv, b * 16 + 16)
                def project_v(i):
                    t = released(("v", i))
                    for s in (2 * i, 2 * i + 1):
                        last = split_product(t[:, HALF * (s % 2):HALF * (s % 2) + HALF],
                                             lambda h, k: (HH, HL)[h][:, k, P * s:P * s + P],
                                             lambda h, k: w_full[0][:, h, k, :], range(KB))
                    last.then_inc(s_big_full, 1)

                def project_qk(j):
                    pair, what, half = j // 4, j % 4 // 2, j % 2
                    if j % 4 == 0:
                        pe.wait_ge(ld_qk[pair], b * 16 + 16)
                    t = released(("qk", j))
                    cols = slice(HALF * half, HALF * half + HALF)
                    split_product(t[:, 0:HALF], lambda h, k: w_qk(pair)[:, h, k, P * what:P * what + P],
                                  lambda h, k: (HH, HL)[h][:, k, cols], range(KB)).then_inc(s_big_full, 1)

                def transposes(u, s):
                    n = 8 * u + s
                    if s == 0:
                        pe.wait_ge(s_p_norm, b * 72 + 4 * u + 4)
                    if n >= 2:
                        pe.wait_ge(s_pt_ready, b * 144 + n - 1)
                    for t in range(4):
                        last = nc.tensor.transpose(tps[n % 2][:, P * t:P * t + P],
                                                   PB[:, 4 * (u % 2) + t, P * s:P * s + P], ident[:])
                    last.then_inc(s_t_full, 1)

                def values0(n):
                    u, s = n // 8, n % 8
                    if s == 0:
                        if u == 0:
                            pe.wait_ge(s_v_ready, b * 4 + 4)
                            pe.wait_ge(s_y_out, b * 8 + CREDIT)
                        elif u == 1:
                            pe.wait_ge(s_y_out, b * 8 + CREDIT)
                        else:
                            pe.wait_ge(s_a_done, b * 16 + u - 1)
                    pe.wait_ge(s_pt_ready, b * 144 + n + 1)
                    for part in range(2):
                        last = mm(ops[u % 2][:], VT[:, s, P * (u // 2):P * (u // 2) + P], pt_slot(u, s)[:, part, :],
                                  start=(s == 0 and part == 0), stop=(s == 7 and part == 1))
                    if s == 7:
                        last.then_inc(s_o_full, 1)

                def scores0(u, tb):
                    head = u // 2 % 2
                    if tb == 0 and u % 2 == 0:
                        pe.wait_ge((s_stack_a, s_stack_b)[head], (b * PAIRS + u // 4 + 1) * 96)
                    t = released(("s", 4 * u + tb))
                    tok = P * (4 * (u % 2) + tb)
                    for half in range(2):
                        cols = slice(HALF * half, HALF * half + HALF)
                        for i, kind in enumerate(("kh", "kl")):
                            last = mm(t[:, cols], stack("q", head)[:, tok:tok + P], stack(kind, head)[:, cols],
                                      start=(i == 0), stop=(i == 1))
                    last.then_inc(s_big_full, 1)

                project_v(0)
                for j in range(4):
                    project_qk(j)
                for i in (1, 2, 3):
                    project_v(i)
                for step in range(STEPS0 + LAG):
                    u, tb, n = step // 4, step % 4, 2 * (step - LAG)
                    if qk_part(step) is not None:
                        project_qk(qk_part(step))
                    if step < STEPS0:
                        scores0(u, tb)
                    if n >= 0:
                        transposes(n // 8, n % 8)
                        transposes(n // 8, n % 8 + 1)
                    if n > 0:
                        values0(n - 2)
                        values0(n - 1)
                values0(8 * UNITS0 - 2)
                values0(8 * UNITS0 - 1)

                pe.wait_ge(s_ld_wp, b * 16 + 16)
                pe.wait_ge(s_a_hi, b * 8 + 6)
                pe.wait_ge(s_a_lo, b * 6 + 6)

                def project_out(t, o, pairs):
                    for half in range(2):
                        if o == 0 and pairs == [PAIRS - 1]:
                            pe.wait_ge(s_a_hi, b * 8 + 7 + half)
                            pe.wait_ge(s_a_lo_last, b * 2 + 1 + half)
                        cols = slice(HALF * half, HALF * half + HALF)
                        for k in pairs:
                            for i, (wp, ap) in enumerate(((0, 0), (0, 1), (1, 0))):
                                last = mm(t[:, cols], w_full[1][:, wp, k, P * o:P * o + P], (HH, HL)[ap][:, k, cols],
                                          start=(k == 0 and i == 0), stop=(k == PAIRS - 1 and i == 2))
                    return last

                tiles = [released(("proj", o)) for o in range(2)]
                for o in range(2):
                    project_out(tiles[o], o, range(PAIRS - 1))
                for o in range(2):
                    project_out(tiles[o], o, [PAIRS - 1]).then_inc(s_big_full, 1)
                for o in (2, 3):
                    project_out(released(("proj", o)), o, range(PAIRS)).then_inc(s_big_full, 1)
                group_means(2 * b + 2, released(("gna", 0)), mv[:, :, 0], s_gn_mean)
                group_means(2 * b + 2, released(("gnb", 0)), wvar, s_gn_var)

                def from_x1(kind, k, slot, blocks=range(KB)):
                    t = released((kind, k))
                    for half in range(2):
                        if kind == "g" and (k or half):
                            pe.wait_ge(s_xc_lo, b * len(XC_PARTS) + k + 2)
                        elif kind == "g":
                            pe.wait_ge(s_xc_lo, b * len(XC_PARTS) + 1)
                        cols = slice(HALF * half, HALF * half + HALF)
                        last = split_product(t[:, cols], lambda h, j: w_full[slot][:, h, j, P * k:P * k + P],
                                             lambda h, j: (HH, HL)[h][:, j, cols], blocks)
                    last.then_inc(s_big_full, 1)

                def project_vp(s):
                    t = released(("u", s))
                    split_product(t[:, 0:HALF], lambda h, k: (HH, HL)[h][:, k, P * s:P * s + P],
                                  lambda h, k: w_full[0][:, h, k, :], range(KB)).then_inc(s_big_full, 1)

                pe.wait_ge(s_ld_g, b * 16 + 16)
                for k in range(KB):
                    from_x1("g", k, 0, range(k + 1))
                pe.wait_ge(s_ld_m, b * 16 + 16)
                from_x1("y", 0, 1)
                from_x1("y", 1, 1)
                t = released(("sum", 0))
                pe.wait_ge(s_prod_sum, b + 1)
                for s in range(NT):
                    last = mm(t[:, s:s + 1], PB[:, 4, P * s:P * s + P], ones[:, 0:1], start=True, stop=True)
                last.then_inc(s_big_full, 1)
                from_x1("y", 2, 1)
                from_x1("y", 3, 1)
                pe.wait_ge(s_ld_u, b * 16 + 16)
                for s in range(3):
                    project_vp(s)
                t = released(("r", 0))
                pe.wait_ge(s_diag_ready, b + 1)
                for half in range(2):
                    cols = slice(HALF * half, HALF * half + HALF)
                    last = mm(t[:, cols], ones[:], PB[:, 0, cols], start=True, stop=True)
                last.then_inc(s_big_full, 1)
                for s in range(3, NT):
                    project_vp(s)

                def scores1(i):
                    t = released(("s1", i))
                    for half in range(2):
                        cols = slice(HALF * half, HALF * half + HALF)
                        last = split_product(t[:, cols], lambda h, k: ST[:, 4 * h + k, P * i:P * i + P],
                                             lambda h, k: (HH, HL)[h][:, k, cols], range(KB))
                    last.then_inc(s_big_full, 1)

                def values1(c, e, s):
                    use = 4 * c + e
                    if s == 0:
                        if use < 2:
                            pe.wait_ge(s_a_done, b * 16 + 16)
                        else:
                            pe.wait_ge(s_y_out, b * 8 + use - 1 + CREDIT)
                    if e < 2:
                        pe.wait_ge(s_pt_ready, b * 144 + 8 * (UNITS0 + c) + s + 1)
                    ptb = pt_slot(UNITS0 + c, s)
                    for i, (vp, pp) in enumerate(((0, 0), (0, 1), (1, 0))):
                        col = HALF * vp + P * e
                        last = mm(ops[use % 2][:], VT[:, s, col:col + P], ptb[:, pp, :],
                                  start=(s == 0 and i == 0), stop=(s == 7 and i == 2))
                    if s == 7:
                        last.then_inc(s_o_full, 1)

                pe.wait_ge(s_y_ready, b * 4 + 4)
                for i in range(4):
                    scores1(i)
                pe.wait_ge(s_vp_ready, b * 8 + 8)
                for c in range(2):
                    for tb in range(4):
                        if c == 0:
                            scores1(4 + tb)
                            if tb == 0 and not last_batch:
                                group_means(2 * b + 3, released(("gna", 1)), mv[:, :, 0], s_gn_mean)
                            if tb == 1 and not last_batch:
                                group_means(2 * b + 3, released(("gnb", 1)), wvar, s_gn_var)
                        transposes(UNITS0 + c, 2 * tb)
                        transposes(UNITS0 + c, 2 * tb + 1)
                        if tb:
                            for s in (2 * tb - 2, 2 * tb - 1):
                                values1(c, 0, s)
                                values1(c, 1, s)
                    for s in (6, 7):
                        values1(c, 0, s)
                        values1(c, 1, s)
                    for e in (2, 3):
                        for s in range(8):
                            values1(c, e, s)

            each_batch(pe, body)

        @block.scalar
        def _(act):
            act_fn = nc.scalar.activation

            for n, j in enumerate((8, 9, 10, 11, 0, 1, 2, 3, 4, 5, 6, 7)):
                if n == 0:
                    act.wait_ge(s_in_l1v, 5 * 16)
                else:
                    act.wait_ge(s_square_sum, n)
                if n == 4:
                    act.wait_ge(s_in_l1, 8 * 16)
                act_fn(RB[:, 0:HALF], w1_block(j), ACT.Square, accum_out=ssq[:, j:j + 1]).then_inc(s_square_sum, 1)
            act.wait_ge(s_in_vout, 16)
            for j in range(4):
                act.wait_ge(s_square_sum, 12 + j)
                act_fn(RB[:, 0:HALF], XA[:, j // 2, HALF * (j % 2):HALF * (j % 2 + 1)], ACT.Square,
                       accum_out=ssq[:, 12 + j:13 + j]).then_inc(s_square_sum, 1)

            def product_hi(i):
                act.wait_ge(s_big_full, i + 1)
                if i == 2 * KB:
                    act.wait_ge(s_const_set, 1)
                for cols, factor in product_parts(i):
                    at = HALF * (i % KB)
                    last = act_fn(product_stage(i // KB)[:, at + cols.start:at + cols.stop], big[i % 2][:, cols],
                                  ACT.Copy, scale=factor)
                last.then_inc(s_prod_hi, 1)

            for i in range(KB):
                product_hi(i)
            act.wait_ge(s_in_l0, 96)
            l0 = [(W[0][:, 0:2048], X[:, 0:2, :]), (W[1][:, 0:2048], X[:, 2:4, :])]
            l0 += [(VT[:, 2 * i, :], XA[:, (2, 3, 0, 1)[i], :]) for i in range(PAIRS)]
            act.wait_ge(s_q_scaled, PAIRS)
            for dst, src in l0:
                act_fn(dst, src if len(src.shape) == 2 else src.rearrange("p a n -> p (a n)"), ACT.Copy)\
                    .then_inc(s_split_hi, 1)
            for i in range(KB, SETUP_BIG):
                product_hi(i)

            def norm_hi(n):
                for k in range(KB):
                    act.wait_ge(s_hn_f, n * 4 + k + 1)
                    act_fn(HH[:, k, :], XA[:, k, :], ACT.Copy).then_inc(s_hn_hi, 1)

            norm_hi(0)

            def body(b, last_batch):
                def full(key):
                    act.wait_ge(s_big_full, big_count(b, key))
                    return big[big_at(b, key) % 2]

                def v_hi(i):
                    t = full(("v", i))
                    act_fn(v_heads(i)[:, :, 0:4:3, :], t[:, :].rearrange("p (q x d) -> p q x d", x=2, d=CH), ACT.Copy)\
                        .then_inc(s_big_hi, 1)

                def qk_hi(j):
                    t = full(("qk", j))
                    pair, what, half = j // 4, j % 4 // 2, j % 2
                    if pair:
                        act.wait_ge(s_stack_a, (b * PAIRS + pair) * 96)
                        act.wait_ge(s_stack_b, (b * PAIRS + pair) * 96)
                    act_fn(unstacked(what, 0)[:, HALF * half:HALF * half + HALF], t[:, 0:HALF], ACT.Identity,
                           bias=(bq, bk)[what][:, pair:pair + 1])\
                        .then_inc(s_big_hi, 1)

                def exps(u, tb):
                    t = full(("s", 4 * u + tb))
                    act.wait_ge(s_row_max, b * 64 + 4 * u + tb + 1)
                    i = 4 * (u % 2) + tb
                    act_fn(PB[:, i, :], t[:], ACT.Exp, bias=negmax[:, i:i + 1], accum_out=rowsum[:, i:i + 1])\
                        .then_inc(s_exp_done, 1)

                def pt_hi(u, s):
                    n = 8 * u + s
                    act.wait_ge(s_t_full, b * 144 + n + 1)
                    act_fn(pt_slot(u, s)[:, 0, :], tps[n % 2][:], ACT.Copy).then_inc(s_pt_hi, 1)

                def corr(u):
                    act.wait_ge(s_o_full, b * 24 + u + 1 + CREDIT)
                    if u:
                        act.wait_ge(s_a_done, b * 16 + u)
                    lo, to = ((64, 0), (0, 64))[u // 2 % 2]
                    act_fn(RB[to:to + 64, 0:HALF], ops[u % 2][lo:lo + 64, :], ACT.Copy).then_inc(s_corr_done, 1)

                def a_hi(pair, half):
                    act.wait_ge(s_a_done, b * 16 + 4 * pair + half + 3)
                    cols = slice(HALF * half, HALF * half + HALF)
                    act_fn(HH[:, pair, cols], XA[:, pair, cols], ACT.Copy).then_inc(s_a_hi, 1)

                v_hi(0)
                for j in range(4):
                    qk_hi(j)
                for i in (1, 2, 3):
                    v_hi(i)
                for step in range(STEPS0 + LAG):
                    u, tb, n = step // 4, step % 4, 2 * (step - LAG)
                    if qk_part(step) is not None:
                        qk_hi(qk_part(step))
                    if n >= 0:
                        pt_hi(n // 8, n % 8)
                        pt_hi(n // 8, n % 8 + 1)
                    if tb == 2 and u >= 2:
                        corr(u - 2)
                    if step < STEPS0:
                        exps(u, tb)
                    for part in a_parts(step):
                        a_hi(*part)
                a_hi(3, 0)
                corr(UNITS0 - 1)
                a_hi(3, 1)
                for o in range(KB):
                    t = full(("proj", o))
                    if o == 0:
                        act.wait_ge(s_a_lo, b * 6 + 6)
                        act.wait_ge(s_a_lo_last, b * 2 + 2)
                    act_fn(XA[:, o, :], t[:], ACT.Identity, bias=bp[:, o:o + 1]).then_inc(s_pr_ready, 1)
                for i, (k, cols) in enumerate(XC_PARTS):
                    act.wait_ge(s_res_sum, b * len(XC_PARTS) + i + 1)
                    if i == 0:
                        act.wait_ge(s_coef_b, b + 1)
                    act_fn(HH[:, k, cols], XA[:, k, cols], ACT.Identity, bias=coefB[:, k:k + 1], scale=RES)\
                        .then_inc(s_xc_hi, 1)
                for k in range(KB):
                    t = full(("y", k))
                    act_fn(ST[:, k, :], t[:], ACT.Copy).then_inc(s_big_hi, 1)
                act.wait_ge(s_diag_ready, b + 1)
                for s in range(NT):
                    t = full(("u", s))
                    act_fn(VT[:, s, 0:HALF], t[:, 0:HALF], ACT.Copy, scale=rcol[:, s:s + 1])\
                        .then_inc(s_big_hi, 1)

                def exps1(i):
                    act.wait_ge(s_neg_ready, b * 8 + i + 1)
                    act_fn(PB[:, i, :], PB[:, i, :], ACT.Exp, bias=negmax[:, i:i + 1], scale=rcol[:, i:i + 1],
                           accum_out=rowsum[:, i:i + 1]).then_inc(s_exp_done, 1)

                for i in range(4):
                    exps1(i)
                for c in range(2):
                    for tb in range(4):
                        pt_hi(UNITS0 + c, 2 * tb)
                        pt_hi(UNITS0 + c, 2 * tb + 1)
                        if c == 0:
                            exps1(4 + tb)
                    if c == 0 and not last_batch:
                        norm_hi(b + 1)

            each_batch(act, body)

        @block.gpsimd
        def _(pool):
            nc.gpsimd.memset(expo[:, 0:8], 0.5)
            nc.gpsimd.memset(expo[:, 8:16], -0.5).then_inc(s_expo_set, 1)
            pool.wait_ge(s_expo_set, 1)
            for n, rows in ((4, slice(8, 12)), (12, slice(0, 8)), (16, slice(12, 16))):
                pool.wait_ge(s_square_sum, n)
                nc.gpsimd.tensor_tensor(rnorm[:, rows], ssq[:, rows], expo[:, 8:8 + rows.stop - rows.start], ALU.pow)\
                  .then_inc(s_norm_pow, 1)
                if n == 4:
                    nc.gpsimd.memset(ones[:], 1.0)
                    nc.gpsimd.memset(product_stage(2).bitcast(f32), 0.0).then_inc(s_const_set, 1)

            def group_rstd(n):
                pool.wait_ge(s_gn_veps, n)
                nc.gpsimd.tensor_tensor(rstd, veps, expo[:, 8:12], ALU.pow).then_inc(s_gn_rstd, 1)

            group_rstd(1)

            def body(b, last_batch):
                def normalise(n):
                    i = n % 8
                    pool.wait_ge(s_recip_done, b * 72 + n + 1)
                    own_wait(pool)
                    nc.gpsimd.tensor_scalar(PB[:, i, :], PB[:, i, :], rinv[:, i:i + 1], 1.0, ALU.mult, ALU.mult)\
                      .then_inc(s_p_norm, 1)

                def a_lo(pair, half):
                    pool.wait_ge(s_a_hi, b * 8 + 2 * pair + half + 1)
                    cols = slice(HALF * half, HALF * half + HALF)
                    nc.gpsimd.tensor_tensor(HL[:, pair, cols], XA[:, pair, cols], HH[:, pair, cols].bitcast(f32),
                                            ALU.subtract).then_inc(s_a_lo, 1)

                for n in range(4 * UNITS0):
                    normalise(n)
                    for part in a_parts(n):
                        a_lo(*part)
                group_rstd(2 * b + 2)
                pool.wait_ge(s_coef_b, b + 1)
                for i, (k, cols) in enumerate(XC_PARTS):
                    pool.wait_ge(s_res_sum, b * len(XC_PARTS) + i + 1)
                    own_wait(pool)
                    nc.gpsimd.tensor_scalar(X[:, k, cols], XA[:, k, cols], RES, coefB[:, k:k + 1], ALU.mult, ALU.add)\
                      .then_inc(s_xc_ready, 1)
                pool.wait_ge(s_ms_done, b + 1)
                nc.gpsimd.tensor_tensor(rms, mean_sq, expo[:, 0:8], ALU.pow).then_inc(s_rms_done, 1)
                for i in range(8):
                    if i == 4:
                        normalise(64 + 3)
                    pool.wait_ge(s_s1_ready, b * 8 + i + 1)
                    own_wait(pool)
                    nc.gpsimd.tensor_scalar(negmax[:, i:i + 1], rowmax1[:, i:i + 1], rcol[:, i:i + 1], -1.0,
                                            ALU.mult, ALU.mult).then_inc(s_neg_ready, 1)
                    if i == 6 and not last_batch:
                        group_rstd(2 * b + 3)
                    if i and i != 4:
                        normalise(64 + i - 1)
                normalise(71)

            each_batch(pool, body)

        @block.vector
        def _(dve):
            V = nc.vector

            links = [0, 0]

            def link(instruction):
                instruction.then_inc(s_dve_step, 1)
                links[1] += 1
                dve.wait_ge(s_dve_step, links[0] + links[1])

            dve.sem_inc(s_y_out, CREDIT)
            dve.wait_ge(s_in_vec, 48)
            for n, rows in ((1, range(8, 12)), (2, range(0, 8))):
                dve.wait_ge(s_norm_pow, n)
                cols = slice(rows.start, rows.stop)
                link(V.tensor_tensor(wscale[:, cols], rnorm[:, cols], g_l1[:, cols], ALU.mult))
                for j in rows:
                    V.tensor_scalar(w1_block(j), w1_block(j), wscale[:, j:j + 1], None, ALU.mult)\
                     .then_inc(s_w_normed, 1)
            link(V.tensor_scalar(bq, bq, SCALE0, None, ALU.mult))

            def product_lo(i):
                dve.wait_ge(s_prod_hi, i + 1)
                for cols, factor in product_parts(i):
                    at = HALF * (i % KB)
                    stage = product_stage(i // KB)
                    last = V.scalar_tensor_tensor(stage[:, 2048 + at + cols.start:2048 + at + cols.stop],
                                                  big[i % 2][:, cols], factor,
                                                  stage[:, at + cols.start:at + cols.stop].bitcast(f32),
                                                  ALU.mult, ALU.subtract)
                last.then_inc(s_prod_lo, 1)

            for i in range(KB):
                product_lo(i)
            dve.wait_ge(s_norm_pow, 3)
            link(V.tensor_tensor(wscale[:, 12:16], rnorm[:, 12:16], g_l1[:, 12:16], ALU.mult))
            link(V.tensor_scalar(wscale[:, 12:16], wscale[:, 12:16], RES, None, ALU.mult))
            dve.wait_ge(s_in_l0, 96)
            for i in range(PAIRS):
                wq = XA[:, i, :].rearrange("p (k n) -> p k n", k=KB)[:, :, 0:P]
                V.tensor_scalar(wq, wq, SCALE0, None, ALU.mult).then_inc(s_q_scaled, 1)
            l0 = [(W[0], X[:, 0:2, :]), (W[1], X[:, 2:4, :])]
            for i, (w, src) in enumerate(l0):
                dve.wait_ge(s_split_hi, i + 1)
                V.tensor_tensor(w[:, 2048:4096], src.rearrange("p a n -> p (a n)"), w[:, 0:2048].bitcast(f32),
                                ALU.subtract).then_inc(s_split_lo, 1)
            for i in range(PAIRS):
                dve.wait_ge(s_split_hi, i + 3)
                V.tensor_tensor(VT[:, 2 * i + 1, :], XA[:, (2, 3, 0, 1)[i], :], VT[:, 2 * i, :].bitcast(f32),
                                ALU.subtract).then_inc(s_split_lo, 1)
            for i in range(KB, 2 * KB):
                product_lo(i)

            def channel_stats(k):
                V.bn_stats(stats[:, k, 0:6], XA[:, k, 0:HALF])
                link(V.bn_stats(stats[:, k, 6:12], XA[:, k, HALF:N]))
                own_wait(dve)
                return V.bn_aggr(mv[:, k, :], stats[:, k, :])

            def group_var(tile, full_at):
                dve.wait_ge(s_big_full, full_at)
                link(V.tensor_copy(gmean, tile[:, 0:KB]))
                link(V.tensor_tensor(dev, mv[:, :, 0], gmean, ALU.subtract))
                link(V.tensor_tensor(dev, dev, dev, ALU.mult))
                V.tensor_tensor(wvar, dev, mv[:, :, 1], ALU.add).then_inc(s_gn_var, 1)

            def group_veps(tile, full_at):
                dve.wait_ge(s_big_full, full_at)
                V.tensor_scalar(veps, tile[:, 0:KB], GN_EPS, None, ALU.add).then_inc(s_gn_veps, 1)

            def group_coefs(n, scale, bias):
                dve.wait_ge(s_gn_rstd, n)
                link(V.tensor_tensor(coefA, rstd, scale, ALU.mult))
                link(V.tensor_tensor(coefT, gmean, coefA, ALU.mult))
                return V.tensor_tensor(coefB, bias, coefT, ALU.subtract)

            def norm_f32():
                for k in range(KB):
                    V.tensor_scalar(XA[:, k, :], XA[:, k, :], coefA[:, k:k + 1], coefB[:, k:k + 1],
                                    ALU.mult, ALU.add).then_inc(s_hn_f, 1)

            def norm_lo(n):
                for k in range(KB):
                    dve.wait_ge(s_hn_hi, n * 4 + k + 1)
                    V.tensor_tensor(HL[:, k, :], XA[:, k, :], HH[:, k, :].bitcast(f32), ALU.subtract)\
                     .then_inc(s_hn_ready, 1)

            dve.wait_ge(s_x_next, 16)
            for k in range(KB):
                last = channel_stats(k)
            last.then_inc(s_gn_mean, 1)
            for i in range(2 * KB, SETUP_BIG):
                product_lo(i)
            dve.wait_ge(s_gn_mean, 1)
            group_var(big[0], SETUP_BIG + 1)
            group_veps(big[1], SETUP_BIG + 2)
            link(group_coefs(1, gs1, gb1))
            norm_f32()
            norm_lo(0)
            links_before = links[1]

            def body(b, last_batch):
                links[0], links[1] = links_before + b * DVE_LINKS, 0

                def at(key):
                    return big_count(b, key)

                def tile(key):
                    return big[big_at(b, key) % 2]

                def v_lo(i):
                    dve.wait_ge(s_big_hi, hi_count(b, ("v", i)))
                    v = v_heads(i)
                    V.tensor_tensor(v[:, :, 1:3, :], tile(("v", i))[:].rearrange("p (q x d) -> p q x d", x=2, d=CH),
                                    v[:, :, 0:4:3, :].bitcast(f32), ALU.subtract).then_inc(s_v_ready, 1)

                def qk_lo(j):
                    pair, what, half = j // 4, j % 4 // 2, j % 2
                    dve.wait_ge(s_big_hi, hi_count(b, ("qk", j)))
                    cols = slice(HALF * half, HALF * half + HALF)
                    V.scalar_tensor_tensor(unstacked(what, 1)[:, cols], tile(("qk", j))[:, 0:HALF],
                                           (bq, bk)[what][:, pair:pair + 1],
                                           unstacked(what, 0)[:, cols].bitcast(f32), ALU.add, ALU.subtract)\
                     .then_inc(s_nat_ready, 1)

                def row_max(u, tb):
                    i = 4 * (u % 2) + tb
                    dve.wait_ge(s_big_full, at(("s", 4 * u + tb)))
                    V.tensor_reduce(negmax[:, i:i + 1], tile(("s", 4 * u + tb))[:], axis=AX.X, op=ALU.max,
                                    negate=True).then_inc(s_row_max, 1)

                def recip(u, tb):
                    i = 4 * (u % 2) + tb
                    dve.wait_ge(s_exp_done, b * 72 + 4 * u + tb + 1)
                    V.reciprocal(rinv[:, i:i + 1], rowsum[:, i:i + 1]).then_inc(s_recip_done, 1)

                def pt_lo(u, s):
                    n = 8 * u + s
                    dve.wait_ge(s_pt_hi, b * 144 + n + 1)
                    V.tensor_tensor(pt_slot(u, s)[:, 1, :], tps[n % 2][:], pt_slot(u, s)[:, 0, :].bitcast(f32),
                                    ALU.subtract).then_inc(s_pt_ready, 1)

                def head_out(u):
                    dve.wait_ge(s_corr_done, b * 16 + u + 1)
                    r = slice(64 * (u // 2 % 2), 64 * (u // 2 % 2) + 64)
                    pair, c = u // 4, u % 2
                    V.scalar_tensor_tensor(XA[r, pair, HALF * c:HALF * c + HALF], ops[u % 2][r, :], bv[r, pair:pair + 1],
                                           RB[r, 0:HALF], ALU.add, ALU.add).then_inc(s_a_done, 1)

                v_lo(0)
                for j in range(4):
                    qk_lo(j)
                for i in (1, 2, 3):
                    v_lo(i)
                for step in range(STEPS0 + LAG):
                    u, tb, n = step // 4, step % 4, 2 * (step - LAG)
                    if qk_part(step) is not None:
                        qk_lo(qk_part(step))
                    if 1 <= step <= STEPS0:
                        recip((step - 1) // 4, (step - 1) % 4)
                    if step < STEPS0:
                        row_max(u, tb)
                    if n >= 0:
                        pt_lo(n // 8, n % 8)
                        pt_lo(n // 8, n % 8 + 1)
                    if tb == 2 and u >= 2:
                        head_out(u - 2)
                for half in range(2):
                    if half:
                        head_out(UNITS0 - 1)
                    dve.wait_ge(s_a_hi, b * 8 + 7 + half)
                    cols = slice(HALF * half, HALF * half + HALF)
                    V.tensor_tensor(HL[:, 3, cols], XA[:, 3, cols], HH[:, 3, cols].bitcast(f32), ALU.subtract)\
                     .then_inc(s_a_lo_last, 1)

                for k in range(KB):
                    dve.wait_ge(s_pr_ready, b * 4 + k + 1)
                    last = channel_stats(k)
                last.then_inc(s_gn_mean, 1)
                dve.wait_ge(s_gn_mean, 2 * b + 2)
                group_var(tile(("gna", 0)), at(("gna", 0)))
                group_veps(tile(("gnb", 0)), at(("gnb", 0)))
                link(group_coefs(2 * b + 2, gs2, gb2))
                V.tensor_scalar(coefB, coefB, RES, None, ALU.mult).then_inc(s_coef_b, 1)
                dve.wait_ge(s_x_res, b * 16 + 16)
                for i, (k, cols) in enumerate(XC_PARTS):
                    V.scalar_tensor_tensor(XA[:, k, cols], XA[:, k, cols], coefA[:, k:k + 1], X[:, k, cols],
                                           ALU.mult, ALU.add).then_inc(s_res_sum, 1)
                    if i >= 2:
                        xc_lo(b, i - 2)
                xc_lo(b, len(XC_PARTS) - 2)
                xc_lo(b, len(XC_PARTS) - 1)

                for k in range(KB):
                    dve.wait_ge(s_big_full, at(("g", k)))
                    V.tensor_tensor(PB[:, 4 + k, :], tile(("g", k))[:], X[:, k, :], ALU.mult)\
                     .then_inc(s_prod_ready, 1)
                    if k:
                        dve.wait_ge(s_prod_ready, b * 4 + k + 1)
                        if k > 1:
                            dve.wait_ge(s_dve_step, links[0] + links[1])
                        total = V.tensor_tensor(PB[:, 4, :], PB[:, 4, :], PB[:, 4 + k, :], ALU.add)
                        if k < KB - 1:
                            total.then_inc(s_dve_step, 1)
                            links[1] += 1
                total.then_inc(s_prod_sum, 1)

                def y_lo(k):
                    dve.wait_ge(s_big_hi, hi_count(b, ("y", k)))
                    V.tensor_tensor(ST[:, 4 + k, :], tile(("y", k))[:], ST[:, k, :].bitcast(f32), ALU.subtract)\
                     .then_inc(s_y_ready, 1)

                def vp_lo(s):
                    dve.wait_ge(s_big_hi, hi_count(b, ("u", s)))
                    V.scalar_tensor_tensor(VT[:, s, HALF:N], tile(("u", s))[:, 0:HALF], rcol[:, s:s + 1],
                                           VT[:, s, 0:HALF].bitcast(f32), ALU.mult, ALU.subtract)\
                     .then_inc(s_vp_ready, 1)

                y_lo(0)
                y_lo(1)
                dve.wait_ge(s_big_full, at(("sum", 0)))
                V.tensor_scalar(mean_sq, tile(("sum", 0))[:, 0:8], 1.0 / (3 * C * RES * RES), 0.0, ALU.mult, ALU.max)\
                 .then_inc(s_ms_done, 1)
                dve.wait_ge(s_rms_done, b + 1)
                link(V.tensor_scalar(rms, rms, RMS_EPS, RES, ALU.add, ALU.mult))
                link(V.reciprocal(rcol, rms))
                for s in range(NT):
                    last = V.tensor_scalar(PB[:, 0, P * s:P * s + P], ident[:], rcol[:, s:s + 1], None, ALU.mult)
                last.then_inc(s_diag_ready, 1)
                y_lo(2)
                y_lo(3)
                for s in range(3):
                    vp_lo(s)
                dve.wait_ge(s_big_full, at(("r", 0)))
                V.tensor_copy(RB[:], tile(("r", 0))[:]).then_inc(s_r_ready, 1)
                for s in range(3, NT):
                    vp_lo(s)

                def scaled_max(i):
                    dve.wait_ge(s_big_full, at(("s1", i)))
                    if i == 0:
                        dve.wait_ge(s_r_ready, b + 1)
                    own_wait(dve)
                    V.tensor_tensor_reduce(out=PB[:, i, :], in0=tile(("s1", i))[:], in1=RB[:], scale=1.0,
                                           scalar=NEG, op0=ALU.mult, op1=ALU.max,
                                           accum_out=rowmax1[:, i:i + 1]).then_inc(s_s1_ready, 1)

                def recip1(i):
                    dve.wait_ge(s_exp_done, b * 72 + 64 + i + 1)
                    V.reciprocal(rinv[:, i:i + 1], rowsum[:, i:i + 1]).then_inc(s_recip_done, 1)

                def layer_out(j):
                    c, e = j // 4, j % 4
                    dve.wait_ge(s_o_full, b * 24 + UNITS0 + j + 1 + CREDIT)
                    xs = X[:, e, HALF * c:HALF * c + HALF]
                    V.scalar_tensor_tensor(xs, ops[j % 2][:], wscale[:, 12 + e:13 + e], xs, ALU.mult, ALU.add)\
                     .then_inc(s_y_out, 1)

                for i in range(4):
                    scaled_max(i)
                    if i:
                        recip1(i - 1)
                    if not last_batch:
                        if i == 0:
                            dve.wait_ge(s_x_next, (b + 2) * 16)
                        last = channel_stats(i)
                if not last_batch:
                    last.then_inc(s_gn_mean, 1)
                recip1(3)
                for tb in range(4):
                    scaled_max(4 + tb)
                    if not last_batch and tb == 0:
                        dve.wait_ge(s_gn_mean, 2 * b + 3)
                        group_var(tile(("gna", 1)), at(("gna", 1)))
                    if not last_batch and tb == 2:
                        group_veps(tile(("gnb", 1)), at(("gnb", 1)))
                    pt_lo(UNITS0, 2 * tb)
                    pt_lo(UNITS0, 2 * tb + 1)
                    recip1(4 + tb)
                    if not last_batch and tb == 2:
                        group_coefs(2 * b + 3, gs1, gb1).then_inc(s_dve_step, 1)
                        links[1] += 1
                layer_out(0)
                layer_out(1)
                if not last_batch:
                    dve.wait_ge(s_dve_step, links[0] + links[1])
                    norm_f32()
                layer_out(2)
                if not last_batch:
                    norm_lo(b + 1)
                layer_out(3)
                for s in range(NT):
                    pt_lo(UNITS0 + 1, s)
                for j in range(4, 8):
                    layer_out(j)
                if not last_batch:
                    assert links[1] == DVE_LINKS, links[1]

            def xc_lo(b, i):
                k, cols = XC_PARTS[i]
                dve.wait_ge(s_xc_hi, b * len(XC_PARTS) + i + 1)
                dve.wait_ge(s_xc_ready, b * len(XC_PARTS) + i + 1)
                V.tensor_tensor(HL[:, k, cols], X[:, k, cols], HH[:, k, cols].bitcast(f32), ALU.subtract)\
                 .then_inc(s_xc_lo, 1)

            each_batch(dve, body)


NEG = -3.0e38


def kernel(**inputs):
    import numpy as np
    import concourse.bacc as bacc
    from concourse.bass_utils import run_bass_kernel_spmd

    nc = bacc.Bacc("TRN2", target_bir_lowering=False, num_devices=1, dynamic_dma_scratch_size=1024)
    g = {k: np.asarray(v) for k, v in inputs.items()}

    def blocks(w_t, cols):
        return np.ascontiguousarray(w_t.reshape(KB, P, cols).transpose(1, 0, 2).reshape(P, KB * cols))

    def columns(v):
        return v.reshape(-1, P).T

    w = g["L0_conv_w_qkv"].reshape(HEADS, 3, CH, C)
    bqkv = g["L0_conv_b_qkv"].reshape(HEADS, 3, CH)
    wqk = [blocks(np.concatenate([w[2 * p:2 * p + 2, j].reshape(P, C) for j in (0, 1)]).T, 2 * P) for p in range(PAIRS)]
    arrays = {
        "x": g["x"].reshape(B, C, N),
        "wv_t": blocks(w[:, 2].reshape(C, C).T, C),
        "wp_t": blocks(g["L0_conv_w_proj"].T, C),
        "wqk_t": np.stack(wqk),
        "v_qkv": g["L1_conv_v_qkv"].reshape(12, P, C),
        "v_out": blocks(g["L1_conv_v_out"], C),
        "wo_t": blocks(g["L1_conv_v_out"].T, C),
        "vecs": np.concatenate([columns(bqkv[:, j].reshape(C)) for j in range(3)]
                               + [columns(g[k]) for k in ("L0_conv_gn1_scale", "L0_conv_gn1_bias", "L0_conv_gn2_scale",
                                                          "L0_conv_gn2_bias", "L0_conv_b_proj", "L1_conv_g_qkv",
                                                          "L1_conv_g_out")], axis=1),
        "consts": np.stack([np.eye(P, dtype=np.float32),
                            np.kron(np.eye(P // 16), np.full((16, 16), 1 / 16)).astype(np.float32)]),
    }
    arrays = {f"in_{k}": np.ascontiguousarray(v) for k, v in arrays.items()}
    aps = [nc.dram_tensor(k, v.shape, f32, kind="ExternalInput").ap() for k, v in arrays.items()]
    out = nc.dram_tensor("out", (B, C, N), f32, kind="ExternalOutput").ap()
    build(nc, *aps, out)
    r = run_bass_kernel_spmd(nc, [arrays], core_ids=[0])
    return r.results[0]["out"].reshape(B, C, 32, 32)
```

```python
import concourse.bass as bass
from concourse import mybir
from contextlib import ExitStack

B, C, N = 8, 512, 1024
HEADS = 8
CH = C // HEADS
P = 128
KB = C // P
NT = N // P
HALF = 512
PAIRS = HEADS // 2
UNITS0 = HEADS * 2
UNITS = UNITS0 + 2
STEPS0 = 4 * UNITS0
GN_EPS = 1e-5
RMS_EPS = 1e-4
RES = 2.0 ** -0.5

f32 = mybir.dt.float32
f32r = mybir.dt.float32r
ACT = mybir.ActivationFunctionType
ALU = mybir.AluOpType
AX = mybir.AxisListType

QK_STEPS = (5, 7, 9, 11)


def qk_part(step):
    if step % 16 in QK_STEPS and step < STEPS0 - 16:
        return 4 * (step // 16 + 1) + QK_STEPS.index(step % 16)
    return None


def a_parts(step):
    return [divmod(i, 2) for i, at in enumerate(A_STEPS) if at == step]


def last_values(step):
    return {0: NT - 2, 3: NT - 1}.get(step)


A_STEPS = (47, 49, 51, 53, 57, 60)
BIG = [("qk", j) for j in range(4)] + [("v", i) for i in range(3)]
for _step in range(STEPS0):
    if qk_part(_step) is not None:
        BIG.append(("qk", qk_part(_step)))
    BIG.append(("s", _step))
BIG += [("proj", k) for k in range(KB)] + [("gna", 0), ("gnb", 0)] + [("g", k) for k in range(KB)]
BIG += [("y", 0), ("y", 1), ("y", 2), ("y", 3), ("u", 0), ("u", 1), ("u", 2), ("r", 0)]
BIG += [("u", s) for s in range(3, NT)] + [("s1", t) for t in range(6)]
BIG += [("gna", 1), ("s1", 6), ("gnb", 1), ("s1", 7)]
NBIG = len(BIG)
assert NBIG % 2 == 0
HI = [key for key in BIG if key[0] in ("v", "qk", "y", "u")]
BIG_LAST = [key for key in BIG if key not in (("gna", 1), ("gnb", 1))]
SETUP_BIG = 3 * KB
BIG_BASE = SETUP_BIG
DVE_LINKS = 16
SCALE0 = float(CH) ** -0.5
SCALE1 = float(C) ** -0.5
XC_PARTS = [(0, slice(0, HALF)), (0, slice(HALF, N))] + [(k, slice(0, N)) for k in range(1, KB)]
LAG = 5
CREDIT = 1


def build(nc, x, wv_t, wp_t, wqk_t, v_qkv, v_out, wo_t, vecs, consts, out):
    ctx = ExitStack()
    with ctx:
        def sb(name, shape, dt=f32):
            return ctx.enter_context(nc.sbuf_tensor(name, shape, dt))

        def ps(name, cols):
            return ctx.enter_context(nc.psum_tensor(name, [P, cols], f32))

        def sem(name):
            return ctx.enter_context(nc.semaphore(name))

        d_wv = nc.dram_tensor("d_wv", [P, 4096], f32)
        d_wp = nc.dram_tensor("d_wp", [P, 4096], f32)
        d_qk = nc.dram_tensor("d_qk", [PAIRS, P, 2048], f32)
        d_g = nc.dram_tensor("d_g", [P, 4096], f32)
        d_m = nc.dram_tensor("d_m", [P, 4096], f32)
        d_u = nc.dram_tensor("d_u", [P, 4096], f32)

        X = sb("X", [P, KB, N])
        XA = sb("XA", [P, KB, N])
        HH = sb("HH", [P, KB, N], f32r)
        HL = sb("HL", [P, KB, N], f32r)
        VT = sb("VT", [P, NT, N], f32r)
        ST = sb("ST", [P, 10, N], f32r)
        PB = sb("PB", [P, 8, N])
        PT = sb("PT", [P, 4, 2, HALF], f32r)
        W = [sb("W0", [P, 4096], f32r), sb("W1", [P, 4096], f32r)]
        RB = sb("RB", [P, N])
        ident = sb("ident", [P, P])
        gavg = sb("gavg", [P, P])
        ones = sb("ones", [P, P])
        vec = sb("vec", [P, 48])
        small = sb("small", [P, 208])
        stats = small[:, 0:48].rearrange("p (k s) -> p k s", k=KB)
        mv = small[:, 48:56].rearrange("p (k s) -> p k s", k=KB)
        gmean, dev, cmean = small[:, 56:60], small[:, 60:64], small[:, 64:68]
        veps, rstd, coefA = small[:, 68:72], small[:, 72:76], small[:, 76:80]
        coefT, coefB = small[:, 80:84], small[:, 84:88]
        negmax, rowsum, rinv = small[:, 88:96], small[:, 96:104], small[:, 104:112]
        mean_sq, rms, rcol = small[:, 112:120], small[:, 120:128], small[:, 128:136]
        rowmax1 = small[:, 136:144]
        ssq, rnorm, wscale = small[:, 144:160], small[:, 160:176], small[:, 176:192]
        expo = small[:, 192:208]
        bq, bk, bv = vec[:, 0:4], vec[:, 4:8], vec[:, 8:12]
        gs1, gb1, gs2, gb2, bp = (vec[:, 12 + 4 * i:16 + 4 * i] for i in range(5))
        g_l1 = vec[:, 32:48]

        big = [ps("big0", N), ps("big1", N)]
        tps = [ps("tps0", HALF), ps("tps1", HALF)]
        ops = [ps("ops0", HALF), ps("ops1", HALF)]

        PT1 = W[1][:, 2048:4096].rearrange("p (s h n) -> p s h n", s=2, h=2)

        def pt_slot(u, s):
            if u < UNITS0:
                return PT[:, s % 4, :, :]
            if s < 4:
                return PT[:, s, :, :]
            return ST[:, s + 4, :].rearrange("p (h n) -> p h n", h=2) if s < 6 else PT1[:, s - 6, :, :]

        def v_heads(start, stop):
            return VT[:, start:stop, :].rearrange("p t n -> p (t n)").rearrange("p (q x d) -> p q x d", x=4, d=CH)

        def stack(kind, head):
            return ST[:, {"q": 0, "kh": 2, "kl": 4}[kind] + head, :]

        def unstacked(kind, part):
            return ST[:, 6 + 2 * kind + part, :]

        w_full = [w[:, :].rearrange("p (h k n) -> p h k n", h=2, k=KB) for w in W]

        def w_qk(pair):
            w = W[1 if pair < 2 else 0][:, 2048 * (pair % 2):2048 * (pair % 2) + 2048]
            return w.rearrange("p (h k n) -> p h k n", h=2, k=KB)

        s_waited = sem("waited")
        s_in_l0 = sem("in_l0")
        s_in_qk = sem("in_qk")
        s_in_l1v = sem("s_in_l1v")
        s_in_wo = sem("in_wo")
        s_in_l1 = sem("in_l1")
        s_in_vout = sem("in_vout")
        s_in_vec = sem("in_vec")
        s_split_hi = sem("split_hi")
        s_split_lo = sem("split_lo")
        s_stored_first = sem("stored_first")
        s_stored_l0 = sem("stored_l0")
        s_square_sum = sem("square_sum")
        s_norm_pow = sem("norm_pow")
        s_w_normed = sem("w_normed")
        s_prod_hi = sem("prod_hi")
        s_prod_lo = sem("prod_lo")
        s_stored_g = sem("stored_g")
        s_dve_step = sem("dve_step")
        s_expo_set = sem("s_expo_set")
        s_const_set = sem("const_set")
        s_x_next = sem("x_next")
        s_x_res = sem("x_res")
        s_ld_wv = sem("ld_wv")
        s_ld_wp = sem("ld_wp")
        s_ld_g = sem("ld_g")
        s_ld_m = sem("ld_m")
        s_ld_u = sem("ld_u")
        s_stack_a = sem("stack_a")
        s_stack_b = sem("stack_b")
        s_out_done = sem("out_done")
        s_big_full = sem("big_full")
        s_big_hi = sem("big_hi")
        s_v_full = sem("v_full")
        s_v_hi = sem("v_hi")
        s_v_ready = sem("v_ready")
        s_nat_ready = sem("nat_ready")
        s_t_full = sem("t_full")
        s_pt_hi = sem("pt_hi")
        s_pt_ready = sem("pt_ready")
        s_o_full = sem("o_full")
        s_row_max = sem("row_max")
        s_exp_done = sem("exp_done")
        s_recip_done = sem("recip_done")
        s_p_norm = sem("p_norm")
        s_corr_done = sem("corr_done")
        s_a_done = sem("a_done")
        s_a_hi = sem("a_hi")
        s_a_lo = sem("a_lo")
        s_a_lo_last = sem("s_a_lo_last")
        s_proj_half = sem("proj_half")
        s_pr_ready = sem("pr_ready")
        s_pr_stats = sem("pr_stats")
        s_gn_mean = sem("gn_mean")
        s_gn_first = sem("gn_first")
        s_gn_var = sem("gn_var")
        s_gn_veps = sem("gn_veps")
        s_gn_rstd = sem("gn_rstd")
        s_coef_b = sem("coef_b")
        s_res_sum = sem("res_sum")
        s_xc_ready = sem("xc_ready")
        s_xc_hi = sem("xc_hi")
        s_xc_lo = sem("xc_lo")
        s_prod_ready = sem("prod_ready")
        s_prod_sum = sem("prod_sum")
        s_sum_full = sem("sum_full")
        s_ms_done = sem("ms_done")
        s_rms_done = sem("rms_done")
        s_diag_ready = sem("diag_ready")
        s_r_ready = sem("r_ready")
        s_y_ready = sem("y_ready")
        s_vp_ready = sem("vp_ready")
        s_s1_ready = sem("s1_ready")
        s_neg_ready = sem("neg_ready")
        s_hn_f = sem("hn_f")
        s_hn_hi = sem("hn_hi")
        s_hn_ready = sem("hn_ready")
        s_y_out = sem("y_out")
        ld_qk = [sem(f"ld_qk{i}") for i in range(PAIRS)]
        block = ctx.enter_context(nc.Block())

        def each_batch(eng, body):
            with eng.Fori(0, B - 1) as b:
                body(b, False)
            body(B - 1, True)

        def w1_block(j, start=0, stop=HALF):
            return PB[:, j // 2, HALF * (j % 2) + start:HALF * (j % 2) + stop]

        def qk_part_of(tile, part):
            return tile.rearrange("p (k n) -> p k n", k=KB)[:, :, P * part:P * part + P]

        def wqk_stage(i):
            return XA[:, (2, 3, 0, 1)[i], :]

        def product_stage(i):
            return (ST[:, 4:8, :].rearrange("p a n -> p (a n)"), PT[:, :, :, :].rearrange("p a h n -> p (a h n)"),
                    ST[:, 0:4, :].rearrange("p a n -> p (a n)"))[i]

        def product_parts(i):
            k = i % KB
            if i // KB == 0:
                return [(slice(0, HALF), 1.0)]
            if i // KB == 1:
                return [(slice(0, HALF), SCALE1)]
            return [(slice(P * k, P * k + P), 1.0)] + ([(slice(P * k + P, HALF), 2.0)] if k < KB - 1 else [])

        def big_at(b, key):
            return (BIG_LAST if isinstance(b, int) else BIG).index(key)

        def big_count(b, key):
            return BIG_BASE + b * NBIG + big_at(b, key) + 1

        def hi_count(b, key):
            return b * len(HI) + HI.index(key) + 1

        def own_wait(eng):
            eng.sem_inc(s_waited, 1)

        def src_x(b):
            return x[b].rearrange("(k p) n -> p k n", p=P)

        @block.sync
        def _(sp):
            sp.sem_inc(s_out_done, 16 * CREDIT)
            sp.dma_start(vec[:], vecs).then_inc(s_in_vec, 16)
            sp.dma_start(ident[:], consts[0]).then_inc(s_in_vec, 16)
            sp.dma_start(gavg[:], consts[1]).then_inc(s_in_vec, 16)
            for j in (8, 9, 10, 11):
                sp.dma_start(w1_block(j), v_qkv[j]).then_inc(s_in_l1v, 16)
            sp.dma_start(PB[:, 6:8, :].rearrange("p a n -> p (a n)"), wo_t).then_inc(s_in_wo, 16)
            for j in range(8):
                sp.dma_start(w1_block(j), v_qkv[j]).then_inc(s_in_l1, 16)
            sp.dma_start(XA[:, 0:2, :].rearrange("p a n -> p (a n)"), v_out).then_inc(s_in_vout, 16)
            sp.dma_start(X[:, 0:2, :].rearrange("p a n -> p (a n)"), wv_t).then_inc(s_in_l0, 16)
            sp.dma_start(X[:, 2:4, :].rearrange("p a n -> p (a n)"), wp_t).then_inc(s_in_l0, 16)
            for i in range(2):
                sp.dma_start(wqk_stage(i), wqk_t[i]).then_inc(s_in_qk, 16)
            sp.wait_ge(s_square_sum, 16)
            for i in range(2, PAIRS):
                sp.dma_start(wqk_stage(i), wqk_t[i]).then_inc(s_in_qk, 16)
            sp.wait_ge(s_split_lo, 6)
            sp.dma_start(XA[:], src_x(0)).then_inc(s_x_next, 16)

            def store_qk(i, done):
                sp.dma_start(d_qk[i], VT[:, 2 * i:2 * i + 2, :].rearrange("p a n -> p (a n)").bitcast(f32)).then_inc(done, 16)

            store_qk(0, s_stored_first)
            sp.dma_start(d_wp[:], W[1][:].bitcast(f32)).then_inc(s_stored_first, 16)
            sp.wait_ge(s_prod_lo, KB)
            sp.dma_start(d_u[:], product_stage(0).bitcast(f32)).then_inc(s_stored_first, 16)
            sp.wait_ge(s_stored_first, 48)
            sp.dma_start(w_qk(0).rearrange("p h k n -> p (h k n)").bitcast(f32), d_qk[0]).then_inc(ld_qk[0], 16)
            sp.dma_start(d_wv[:], W[0][:].bitcast(f32)).then_inc(s_stored_l0, 16)
            for i in range(1, PAIRS):
                store_qk(i, s_stored_l0)
            sp.wait_ge(s_prod_lo, 2 * KB)
            sp.dma_start(d_m[:], product_stage(1).bitcast(f32)).then_inc(s_stored_l0, 16)
            sp.wait_ge(s_stored_l0, 80)
            sp.sem_inc(s_ld_wv, 16)
            sp.wait_ge(s_prod_lo, 3 * KB)
            sp.dma_start(d_g[:], product_stage(2).bitcast(f32)).then_inc(s_stored_g, 16)
            sp.wait_ge(s_stored_g, 16)

            def stack_head(b, pair, head):
                rows = slice(64 * head, 64 * head + 64)
                s_stack = (s_stack_a, s_stack_b)[head]
                sp.wait_ge(s_nat_ready, b * 16 + 4 * pair + 4)
                own_wait(sp)
                if pair:
                    sp.wait_ge(s_big_full, big_count(b, ("s", 16 * (pair - 1) + 8 * head + 7)))
                    own_wait(sp)
                moves = [("q", 64 * head, 0, 0), ("q", 64 - 64 * head, 0, 1)]
                moves += [("kh", q, 1, 0) for q in (0, 64)] + [("kl", q, 1, 1) for q in (0, 64)]
                for kind, to, what, part in moves:
                    sp.dma_start(stack(kind, head)[to:to + 64, :].bitcast(f32),
                                 unstacked(what, part)[rows, :].bitcast(f32))\
                      .then_inc(s_stack, 16)

            def body(b, last):
                sp.wait_ge(s_o_full, b * 24 + CREDIT)
                own_wait(sp)
                sp.dma_start(w_qk(1).rearrange("p h k n -> p (h k n)").bitcast(f32), d_qk[1]).then_inc(ld_qk[1], 16)
                stack_head(b, 0, 0)
                stack_head(b, 0, 1)
                sp.wait_ge(s_out_done, (b * 8 + CREDIT) * 16)
                own_wait(sp)
                sp.dma_start(X[:], src_x(b)).then_inc(s_x_res, 16)
                sp.wait_ge(s_v_full, b * 2 + 2)
                own_wait(sp)
                for i in (2, 3):
                    sp.dma_start(w_qk(i).rearrange("p h k n -> p (h k n)").bitcast(f32), d_qk[i]).then_inc(ld_qk[i], 16)
                stack_head(b, 1, 0)
                sp.dma_start(W[1][:].bitcast(f32), d_wp[:]).then_inc(s_ld_wp, 16)
                stack_head(b, 1, 1)
                stack_head(b, 2, 0)
                stack_head(b, 2, 1)
                stack_head(b, 3, 0)
                sp.dma_start(W[0][:].bitcast(f32), d_g[:]).then_inc(s_ld_g, 16)
                stack_head(b, 3, 1)
                sp.wait_ge(s_big_full, big_count(b, ("proj", KB - 1)))
                own_wait(sp)
                sp.dma_start(W[1][:].bitcast(f32), d_m[:]).then_inc(s_ld_m, 16)
                if not last:
                    sp.wait_ge(s_xc_ready, (b + 1) * len(XC_PARTS))
                    sp.wait_ge(s_xc_hi, (b + 1) * len(XC_PARTS))
                    own_wait(sp)
                    sp.dma_start(XA[:], src_x(b + 1)).then_inc(s_x_next, 16)
                sp.wait_ge(s_big_full, big_count(b, ("g", KB - 1)))
                own_wait(sp)
                sp.dma_start(W[0][:].bitcast(f32), d_u[:]).then_inc(s_ld_u, 16)
                if not last:
                    sp.wait_ge(s_big_full, big_count(b, ("y", KB - 1)))
                    own_wait(sp)
                    sp.dma_start(w_qk(0).rearrange("p h k n -> p (h k n)").bitcast(f32), d_qk[0])\
                      .then_inc(ld_qk[0], 16)
                    sp.wait_ge(s_big_full, big_count(b, ("u", NT - 1)))
                    own_wait(sp)
                    sp.dma_start(W[0][:].bitcast(f32), d_wv[:]).then_inc(s_ld_wv, 16)
                for j in range(8):
                    sp.wait_ge(s_y_out, b * 8 + j + 1 + CREDIT)
                    own_wait(sp)
                    c, e = j // 4, j % 4
                    sp.dma_start(out[b].rearrange("(k p) n -> p k n", p=P)[:, e, HALF * c:HALF * c + HALF],
                                 X[:, e, HALF * c:HALF * c + HALF]).then_inc(s_out_done, 16)

            each_batch(sp, body)
            sp.wait_ge(s_out_done, (B * 8 + CREDIT) * 16)

        @block.tensor
        def _(pe):
            mm = nc.tensor.matmul

            def split_product(dst, stat, mov, ks):
                n, i = 3 * len(ks), 0
                for k in ks:
                    for sp_, mp_ in ((0, 0), (0, 1), (1, 0)):
                        last = mm(dst, stat(sp_, k), mov(mp_, k), start=(i == 0), stop=(i == n - 1))
                        i += 1
                return last

            def group_means(n, tile, bias, done):
                pe.wait_ge(s_gn_mean, n)
                last = mm(tile[:, 0:KB], gavg[:], mv[:, :, 0], start=True, stop=bias is None)
                if bias is not None:
                    last = mm(tile[:, 0:KB], gavg[:], bias, start=False, stop=True)
                last.then_inc(done, 1)

            def group_vars(n, tile, done):
                mm(tile[:, 0:KB], gavg[:], mv[:, :, 1], start=True, stop=False)
                pe.wait_ge(s_gn_var, n)
                mm(tile[:, 0:KB], gavg[:], dev, start=False, stop=True).then_inc(done, 1)

            pe.sem_inc(s_o_full, CREDIT)
            pe.wait_ge(s_in_wo, 16)
            pe.wait_ge(s_w_normed, 4)
            for i in range(KB):
                if i >= 2:
                    pe.wait_ge(s_prod_lo, i - 1)
                for j in range(4):
                    last = mm(big[i % 2][:, 0:HALF], w1_block(8 + j, P * i, P * i + P),
                              PB[:, 6 + j // 2, HALF * (j % 2):HALF * (j % 2 + 1)], start=(j == 0), stop=(j == 3))
                last.then_inc(s_big_full, 1)
            pe.wait_ge(s_w_normed, 12)
            for i in range(KB):
                pe.wait_ge(s_prod_lo, KB + i - 1)
                for j in range(4):
                    last = mm(big[i % 2][:, 0:HALF], w1_block(j, P * i, P * i + P), w1_block(4 + j),
                              start=(j == 0), stop=(j == 3))
                last.then_inc(s_big_full, 1)
            for i in range(KB):
                pe.wait_ge(s_prod_lo, 2 * KB + i - 1)
                for j in range(12):
                    last = mm(big[i % 2][:, P * i:HALF], w1_block(j, P * i, P * i + P), w1_block(j, P * i),
                              start=(j == 0), stop=(j == 11))
                last.then_inc(s_big_full, 1)
                if i == 0:
                    pe.wait_ge(s_in_vec, 48)
                    group_means(1, ops[0], None, s_gn_first)
                if i == 1:
                    group_vars(1, ops[1], s_gn_first)
            pe.wait_ge(s_const_set, 1)
            pe.wait_ge(s_prod_lo, SETUP_BIG)

            def body(b, last_batch):
                def released(key):
                    i = big_at(b, key)
                    if i >= 2:
                        kind, k = (BIG_LAST if last_batch else BIG)[i - 2]
                        reader, per = {"v": (s_v_ready, 5), "qk": (s_nat_ready, 16), "s": (s_exp_done, 72),
                                       "proj": (s_pr_ready, 4), "gna": (s_gn_var, 2), "gnb": (s_gn_veps, 2),
                                       "g": (s_prod_ready, 4), "r": (s_r_ready, 1),
                                       "y": (s_y_ready, 4), "u": (s_vp_ready, 8), "s1": (s_s1_ready, 8)}[kind]
                        pe.wait_ge(reader, b * per + k + (2 if kind in ("gna", "gnb") else 1))
                    return big[i % 2]

                pe.wait_ge(s_hn_ready, b * KB + KB)

                def project_v(i):
                    t = released(("v", i))
                    for s in (2 * i, 2 * i + 1):
                        last = split_product(t[:, HALF * (s % 2):HALF * (s % 2) + HALF],
                                             lambda h, k: (HH, HL)[h][:, k, P * s:P * s + P],
                                             lambda h, k: w_full[0][:, h, k, :], range(KB))
                    last.then_inc(s_big_full, 1)

                def project_last_v(s):
                    if s == NT - 2:
                        pe.wait_ge(s_y_out, b * 8 + CREDIT)
                    split_product(ops[s % 2][:], lambda h, k: (HH, HL)[h][:, k, P * s:P * s + P],
                                  lambda h, k: w_full[0][:, h, k, :], range(KB)).then_inc(s_v_full, 1)

                def project_qk(j):
                    pair, what, half = j // 4, j % 4 // 2, j % 2
                    if j % 4 == 0:
                        pe.wait_ge(ld_qk[pair], b * 16 + 16)
                    t = released(("qk", j))
                    cols = slice(HALF * half, HALF * half + HALF)
                    split_product(t[:, 0:HALF], lambda h, k: w_qk(pair)[:, h, k, P * what:P * what + P],
                                  lambda h, k: (HH, HL)[h][:, k, cols], range(KB)).then_inc(s_big_full, 1)

                def transposes(u, s):
                    n = 8 * u + s
                    if s == 0:
                        pe.wait_ge(s_p_norm, b * 72 + 4 * u + 4)
                    if n >= 2:
                        pe.wait_ge(s_pt_ready, b * 144 + n - 1)
                    for t in range(4):
                        last = nc.tensor.transpose(tps[n % 2][:, P * t:P * t + P],
                                                   PB[:, 4 * (u % 2) + t, P * s:P * s + P], ident[:])
                    last.then_inc(s_t_full, 1)

                def values0(n):
                    u, s = n // 8, n % 8
                    if s == 0:
                        if u == 0:
                            pe.wait_ge(s_v_ready, b * 5 + 5)
                        elif u > 1:
                            pe.wait_ge(s_corr_done, b * 16 + u - 1)
                    pe.wait_ge(s_pt_ready, b * 144 + n + 1)
                    for part in range(2):
                        last = mm(ops[u % 2][:], VT[:, s, P * (u // 2):P * (u // 2) + P], pt_slot(u, s)[:, part, :],
                                  start=(s == 0 and part == 0), stop=(s == 7 and part == 1))
                    if s == 7:
                        last.then_inc(s_o_full, 1)

                def scores0(u, tb):
                    head = u // 2 % 2
                    if tb == 0 and u % 2 == 0:
                        pe.wait_ge((s_stack_a, s_stack_b)[head], (b * PAIRS + u // 4 + 1) * 96)
                    t = released(("s", 4 * u + tb))
                    tok = P * (4 * (u % 2) + tb)
                    for half in range(2):
                        cols = slice(HALF * half, HALF * half + HALF)
                        for i, kind in enumerate(("kh", "kl")):
                            last = mm(t[:, cols], stack("q", head)[:, tok:tok + P], stack(kind, head)[:, cols],
                                      start=(i == 0), stop=(i == 1))
                    last.then_inc(s_big_full, 1)

                for j in range(4):
                    project_qk(j)
                pe.wait_ge(s_ld_wv, b * 16 + 16)
                for i in range(3):
                    project_v(i)
                for step in range(STEPS0 + LAG):
                    u, tb, n = step // 4, step % 4, 2 * (step - LAG)
                    if qk_part(step) is not None:
                        project_qk(qk_part(step))
                    if step < STEPS0:
                        scores0(u, tb)
                    if last_values(step):
                        project_last_v(last_values(step))
                    if n >= 0:
                        transposes(n // 8, n % 8)
                        transposes(n // 8, n % 8 + 1)
                    if n > 0:
                        values0(n - 2)
                        values0(n - 1)
                values0(8 * UNITS0 - 2)
                values0(8 * UNITS0 - 1)

                pe.wait_ge(s_ld_wp, b * 16 + 16)
                pe.wait_ge(s_a_hi, b * 8 + 6)
                pe.wait_ge(s_a_lo, b * 6 + 6)

                def project_out(t, o, pairs):
                    for half in range(2):
                        if o == 0 and pairs == [PAIRS - 1]:
                            pe.wait_ge(s_a_hi, b * 8 + 7 + half)
                            pe.wait_ge(s_a_lo_last, b * 2 + 1 + half)
                        cols = slice(HALF * half, HALF * half + HALF)
                        for k in pairs:
                            for i, (wp, ap) in enumerate(((0, 0), (0, 1), (1, 0))):
                                last = mm(t[:, cols], w_full[1][:, wp, k, P * o:P * o + P], (HH, HL)[ap][:, k, cols],
                                          start=(k == 0 and i == 0), stop=(k == PAIRS - 1 and i == 2))
                        if half == 0 and pairs[-1] == PAIRS - 1:
                            last.then_inc(s_proj_half, 1)
                    return last

                tiles = [released(("proj", o)) for o in range(2)]
                for o in range(2):
                    project_out(tiles[o], o, range(PAIRS - 1))
                for o in range(2):
                    project_out(tiles[o], o, [PAIRS - 1]).then_inc(s_big_full, 1)
                for o in (2, 3):
                    project_out(released(("proj", o)), o, range(PAIRS)).then_inc(s_big_full, 1)
                group_means(2 * b + 2, released(("gna", 0)), bp, s_big_full)
                group_vars(2 * b + 2, released(("gnb", 0)), s_big_full)

                def from_x1(kind, k, slot, blocks=range(KB)):
                    t = released((kind, k))
                    for half in range(2):
                        if kind == "g" and (k or half):
                            pe.wait_ge(s_xc_lo, b * len(XC_PARTS) + k + 2)
                        elif kind == "g":
                            pe.wait_ge(s_xc_lo, b * len(XC_PARTS) + 1)
                        cols = slice(HALF * half, HALF * half + HALF)
                        last = split_product(t[:, cols], lambda h, j: w_full[slot][:, h, j, P * k:P * k + P],
                                             lambda h, j: (HH, HL)[h][:, j, cols], blocks)
                    last.then_inc(s_big_full, 1)

                def project_vp(s):
                    t = released(("u", s))
                    split_product(t[:, 0:HALF], lambda h, k: (HH, HL)[h][:, k, P * s:P * s + P],
                                  lambda h, k: w_full[0][:, h, k, :], range(KB)).then_inc(s_big_full, 1)

                pe.wait_ge(s_ld_g, b * 16 + 16)
                for k in range(KB):
                    from_x1("g", k, 0, range(k + 1))
                pe.wait_ge(s_ld_m, b * 16 + 16)
                from_x1("y", 0, 1)
                from_x1("y", 1, 1)
                t = ops[0]
                pe.wait_ge(s_a_done, b * 16 + 16)
                pe.wait_ge(s_prod_sum, b + 1)
                for s in range(NT):
                    last = mm(t[:, s:s + 1], PB[:, 4, P * s:P * s + P], ones[:, 0:1], start=True, stop=True)
                last.then_inc(s_sum_full, 1)
                from_x1("y", 2, 1)
                from_x1("y", 3, 1)
                pe.wait_ge(s_ld_u, b * 16 + 16)
                for s in range(3):
                    project_vp(s)
                t = released(("r", 0))
                pe.wait_ge(s_diag_ready, b + 1)
                for half in range(2):
                    cols = slice(HALF * half, HALF * half + HALF)
                    last = mm(t[:, cols], ones[:], PB[:, 0, cols], start=True, stop=True)
                last.then_inc(s_big_full, 1)
                for s in range(3, NT):
                    project_vp(s)

                def scores1(i):
                    t = released(("s1", i))
                    for half in range(2):
                        cols = slice(HALF * half, HALF * half + HALF)
                        last = split_product(t[:, cols], lambda h, k: ST[:, 4 * h + k, P * i:P * i + P],
                                             lambda h, k: (HH, HL)[h][:, k, cols], range(KB))
                    last.then_inc(s_big_full, 1)

                def values1(c, e, s):
                    use = 4 * c + e
                    if s == 0:
                        if use >= 2:
                            pe.wait_ge(s_y_out, b * 8 + use - 1 + CREDIT)
                    if e < 2:
                        pe.wait_ge(s_pt_ready, b * 144 + 8 * (UNITS0 + c) + s + 1)
                    ptb = pt_slot(UNITS0 + c, s)
                    for i, (vp, pp) in enumerate(((0, 0), (0, 1), (1, 0))):
                        col = HALF * vp + P * e
                        last = mm(ops[use % 2][:], VT[:, s, col:col + P], ptb[:, pp, :],
                                  start=(s == 0 and i == 0), stop=(s == 7 and i == 2))
                    if s == 7:
                        last.then_inc(s_o_full, 1)

                pe.wait_ge(s_y_ready, b * 4 + 4)
                for i in range(4):
                    scores1(i)
                pe.wait_ge(s_vp_ready, b * 8 + 8)
                for c in range(2):
                    for tb in range(4):
                        if c == 0:
                            scores1(4 + tb)
                        if (c, tb) != (1, 0):
                            transposes(UNITS0 + c, 2 * tb)
                            transposes(UNITS0 + c, 2 * tb + 1)
                        if tb:
                            for s in (2 * tb - 2, 2 * tb - 1):
                                values1(c, 0, s)
                                values1(c, 1, s)
                        if (c, tb) == (0, 1) and not last_batch:
                            group_means(2 * b + 3, released(("gna", 1)), None, s_big_full)
                        if (c, tb) == (0, 2) and not last_batch:
                            group_vars(2 * b + 3, released(("gnb", 1)), s_big_full)
                    for e in (0, 1):
                        values1(c, e, 6)
                        values1(c, e, 7)
                    for e in (2, 3):
                        for s in range(8):
                            if (c, e, s) == (0, 3, 6):
                                transposes(UNITS0 + 1, 0)
                                transposes(UNITS0 + 1, 1)
                            values1(c, e, s)

            each_batch(pe, body)

        @block.scalar
        def _(act):
            act_fn = nc.scalar.activation

            def square_sums(n, src, col):
                if n > 1:
                    act.wait_ge(s_square_sum, n - 1)
                act_fn(RB[:, 0:HALF], src, ACT.Square, accum_out=ssq[:, col:col + 1]).then_inc(s_square_sum, 1)

            def product_hi(i):
                act.wait_ge(s_big_full, i + 1)
                if i == 2 * KB:
                    act.wait_ge(s_const_set, 1)
                for cols, factor in product_parts(i):
                    at = HALF * (i % KB)
                    last = act_fn(product_stage(i // KB)[:, at + cols.start:at + cols.stop], big[i % 2][:, cols],
                                  ACT.Copy, scale=factor)
                last.then_inc(s_prod_hi, 1)

            act.wait_ge(s_in_l1v, 4 * 16)
            for j in range(4):
                square_sums(j + 1, w1_block(8 + j), 8 + j)
            act.wait_ge(s_in_l1, 8 * 16)
            for j in range(8):
                square_sums(j + 5, w1_block(j), j)
                if j == 4:
                    product_hi(0)
            product_hi(1)
            act.wait_ge(s_in_vout, 16)
            for j in range(4):
                square_sums(j + 13, XA[:, j // 2, HALF * (j % 2):HALF * (j % 2 + 1)], 12 + j)
            product_hi(2)
            product_hi(3)
            act.wait_ge(s_in_l0, 32)
            for w, src in ((W[0], X[:, 0:2, :]), (W[1], X[:, 2:4, :])):
                act_fn(w[:, 0:2048], src.rearrange("p a n -> p (a n)"), ACT.Copy).then_inc(s_split_hi, 1)
            act.wait_ge(s_in_qk, 16 * PAIRS)
            for i in range(PAIRS):
                if i % 2 == 0:
                    product_hi(KB + i // 2)
                for part, factor in ((0, SCALE0), (1, 1.0)):
                    last = act_fn(qk_part_of(VT[:, 2 * i, :], part), qk_part_of(wqk_stage(i), part),
                                  ACT.Copy, scale=factor)
                last.then_inc(s_split_hi, 1)
            product_hi(KB + 2)
            product_hi(KB + 3)
            product_hi(2 * KB)
            product_hi(2 * KB + 1)

            def norm_hi(n):
                for k in range(KB):
                    act.wait_ge(s_hn_f, n * 4 + k + 1)
                    act_fn(HH[:, k, :], XA[:, k, :], ACT.Copy).then_inc(s_hn_hi, 1)

            norm_hi(0)
            product_hi(2 * KB + 2)
            product_hi(2 * KB + 3)

            def body(b, last_batch):
                def full(key):
                    act.wait_ge(s_big_full, big_count(b, key))
                    return big[big_at(b, key) % 2]

                def v_hi(i):
                    t = full(("v", i))
                    act_fn(v_heads(2 * i, 2 * i + 2)[:, :, 0:4:3, :], t[:, :].rearrange("p (q x d) -> p q x d", x=2, d=CH), ACT.Copy)\
                        .then_inc(s_big_hi, 1)

                def last_v_hi(s):
                    act.wait_ge(s_v_full, b * 2 + s - 5)
                    act_fn(v_heads(s, s + 1)[:, :, 0:4:3, :], ops[s % 2][:].rearrange("p (q x d) -> p q x d", x=2, d=CH),
                           ACT.Copy).then_inc(s_v_hi, 1)

                def qk_hi(j):
                    t = full(("qk", j))
                    pair, what, half = j // 4, j % 4 // 2, j % 2
                    if pair:
                        act.wait_ge(s_stack_a, (b * PAIRS + pair) * 96)
                        act.wait_ge(s_stack_b, (b * PAIRS + pair) * 96)
                    act_fn(unstacked(what, 0)[:, HALF * half:HALF * half + HALF], t[:, 0:HALF], ACT.Identity,
                           bias=(bq, bk)[what][:, pair:pair + 1])\
                        .then_inc(s_big_hi, 1)

                def exps(u, tb):
                    t = full(("s", 4 * u + tb))
                    act.wait_ge(s_row_max, b * 64 + 4 * u + tb + 1)
                    i = 4 * (u % 2) + tb
                    act_fn(PB[:, i, :], t[:], ACT.Exp, bias=negmax[:, i:i + 1], accum_out=rowsum[:, i:i + 1])\
                        .then_inc(s_exp_done, 1)

                def pt_hi(u, s):
                    n = 8 * u + s
                    act.wait_ge(s_t_full, b * 144 + n + 1)
                    act_fn(pt_slot(u, s)[:, 0, :], tps[n % 2][:], ACT.Copy).then_inc(s_pt_hi, 1)

                def corr(u, part):
                    if part == 0:
                        act.wait_ge(s_o_full, b * 24 + u + 1 + CREDIT)
                        if u:
                            act.wait_ge(s_a_done, b * 16 + u)
                    lo, to = ((64, 0), (0, 64))[u // 2 % 2]
                    if part == 0:
                        act_fn(RB[to:to + 64, 0:HALF], ops[u % 2][lo:lo + 64, :], ACT.Copy)
                    else:
                        act_fn(RB[to:to + 64, HALF:N], ops[u % 2][to:to + 64, :], ACT.Identity,
                               bias=bv[to:to + 64, u // 4:u // 4 + 1]).then_inc(s_corr_done, 1)

                def a_hi(pair, half):
                    act.wait_ge(s_a_done, b * 16 + 4 * pair + half + 3)
                    cols = slice(HALF * half, HALF * half + HALF)
                    act_fn(HH[:, pair, cols], XA[:, pair, cols], ACT.Copy).then_inc(s_a_hi, 1)

                for j in range(4):
                    qk_hi(j)
                for i in range(3):
                    v_hi(i)
                for step in range(STEPS0 + LAG):
                    u, tb, n = step // 4, step % 4, 2 * (step - LAG)
                    if qk_part(step) is not None:
                        qk_hi(qk_part(step))
                    if n >= 0:
                        pt_hi(n // 8, n % 8)
                        pt_hi(n // 8, n % 8 + 1)
                    if tb == 2 and u >= 2:
                        corr(u - 2, 0)
                    if tb == 0 and u >= 3:
                        corr(u - 3, 1)
                    if step < STEPS0:
                        exps(u, tb)
                    if last_values(step):
                        last_v_hi(last_values(step))
                    for part in a_parts(step):
                        a_hi(*part)
                a_hi(3, 0)
                corr(UNITS0 - 1, 0)
                corr(UNITS0 - 1, 1)
                a_hi(3, 1)
                for o in range(KB):
                    t = full(("proj", o))
                    if o == 0:
                        act.wait_ge(s_a_lo, b * 6 + 6)
                        act.wait_ge(s_a_lo_last, b * 2 + 2)
                    for half in range(2):
                        act.wait_ge(s_pr_stats, b * 8 + 2 * o + half + 1)
                        cols = slice(HALF * half, HALF * half + HALF)
                        last = act_fn(XA[:, o, cols], t[:, cols], ACT.Identity, bias=bp[:, o:o + 1])
                    last.then_inc(s_pr_ready, 1)
                for i, (k, cols) in enumerate(XC_PARTS):
                    act.wait_ge(s_res_sum, b * len(XC_PARTS) + i + 1)
                    if i == 0:
                        act.wait_ge(s_coef_b, b + 1)
                    act_fn(HH[:, k, cols], XA[:, k, cols], ACT.Identity, bias=coefB[:, k:k + 1], scale=RES)\
                        .then_inc(s_xc_hi, 1)
                for k in range(KB):
                    t = full(("y", k))
                    act_fn(ST[:, k, :], t[:], ACT.Copy).then_inc(s_big_hi, 1)
                act.wait_ge(s_diag_ready, b + 1)
                for s in range(NT):
                    t = full(("u", s))
                    act_fn(VT[:, s, 0:HALF], t[:, 0:HALF], ACT.Copy, scale=rcol[:, s:s + 1])\
                        .then_inc(s_big_hi, 1)

                def exps1(i):
                    act.wait_ge(s_neg_ready, b * 8 + i + 1)
                    act_fn(PB[:, i, :], PB[:, i, :], ACT.Exp, bias=negmax[:, i:i + 1], scale=rcol[:, i:i + 1],
                           accum_out=rowsum[:, i:i + 1]).then_inc(s_exp_done, 1)

                for i in range(4):
                    exps1(i)
                for c in range(2):
                    for tb in range(4):
                        pt_hi(UNITS0 + c, 2 * tb)
                        pt_hi(UNITS0 + c, 2 * tb + 1)
                        if c == 0:
                            exps1(4 + tb)
                    if c == 0 and not last_batch:
                        norm_hi(b + 1)

            each_batch(act, body)

        @block.gpsimd
        def _(pool):
            nc.gpsimd.memset(expo[:, 0:8], 0.5)
            nc.gpsimd.memset(expo[:, 8:16], -0.5).then_inc(s_expo_set, 1)
            pool.wait_ge(s_expo_set, 1)
            for n, rows in ((4, slice(8, 12)), (12, slice(0, 8)), (16, slice(12, 16))):
                pool.wait_ge(s_square_sum, n)
                nc.gpsimd.tensor_tensor(rnorm[:, rows], ssq[:, rows], expo[:, 8:8 + rows.stop - rows.start], ALU.pow)\
                  .then_inc(s_norm_pow, 1)
                if n == 4:
                    nc.gpsimd.memset(ones[:], 1.0)
                    nc.gpsimd.memset(product_stage(2).bitcast(f32), 0.0).then_inc(s_const_set, 1)

            def group_rstd(n):
                pool.wait_ge(s_gn_veps, n)
                nc.gpsimd.tensor_tensor(rstd, veps, expo[:, 8:12], ALU.pow).then_inc(s_gn_rstd, 1)

            group_rstd(1)

            def body(b, last_batch):
                def normalise(n):
                    i = n % 8
                    pool.wait_ge(s_recip_done, b * 72 + n + 1)
                    own_wait(pool)
                    nc.gpsimd.tensor_scalar(PB[:, i, :], PB[:, i, :], rinv[:, i:i + 1], 1.0, ALU.mult, ALU.mult)\
                      .then_inc(s_p_norm, 1)

                def head_out(u):
                    pool.wait_ge(s_corr_done, b * 16 + u + 1)
                    pool.wait_ge(s_p_norm, b * 72 + min(4 * u + 12, 4 * UNITS0))
                    if u == UNITS0 - 2:
                        pool.wait_ge(s_a_lo, b * 6 + 6)
                    rows, pair, c = slice(64 * (u // 2 % 2), 64 * (u // 2 % 2) + 64), u // 4, u % 2
                    nc.gpsimd.tensor_tensor(XA[rows, pair, HALF * c:HALF * c + HALF], RB[rows, 0:HALF],
                                            RB[rows, HALF:N], ALU.add).then_inc(s_a_done, 1)
                    pool.wait_ge(s_a_done, b * 16 + u + 1)
                    own_wait(pool)

                def a_lo(pair, half):
                    pool.wait_ge(s_a_hi, b * 8 + 2 * pair + half + 1)
                    cols = slice(HALF * half, HALF * half + HALF)
                    nc.gpsimd.tensor_tensor(HL[:, pair, cols], XA[:, pair, cols], HH[:, pair, cols].bitcast(f32),
                                            ALU.subtract).then_inc(s_a_lo, 1)

                for n in range(4 * UNITS0):
                    normalise(n)
                    if n % 4 == 3 and n >= 8:
                        head_out(n // 4 - 2)
                    for part in a_parts(n):
                        a_lo(*part)
                head_out(UNITS0 - 2)
                head_out(UNITS0 - 1)
                group_rstd(2 * b + 2)
                pool.wait_ge(s_coef_b, b + 1)
                for i, (k, cols) in enumerate(XC_PARTS):
                    pool.wait_ge(s_res_sum, b * len(XC_PARTS) + i + 1)
                    own_wait(pool)
                    nc.gpsimd.tensor_scalar(X[:, k, cols], XA[:, k, cols], RES, coefB[:, k:k + 1], ALU.mult, ALU.add)\
                      .then_inc(s_xc_ready, 1)
                pool.wait_ge(s_ms_done, b + 1)
                nc.gpsimd.tensor_tensor(rms, mean_sq, expo[:, 0:8], ALU.pow).then_inc(s_rms_done, 1)
                for i in range(8):
                    if i == 4:
                        normalise(64 + 3)
                    pool.wait_ge(s_s1_ready, b * 8 + i + 1)
                    own_wait(pool)
                    nc.gpsimd.tensor_scalar(negmax[:, i:i + 1], rowmax1[:, i:i + 1], rcol[:, i:i + 1], -1.0,
                                            ALU.mult, ALU.mult).then_inc(s_neg_ready, 1)
                    if i == 7 and not last_batch:
                        group_rstd(2 * b + 3)
                    if i and i != 4:
                        normalise(64 + i - 1)
                normalise(71)

            each_batch(pool, body)

        @block.vector
        def _(dve):
            V = nc.vector

            links = [0, 0]

            def link(instruction):
                instruction.then_inc(s_dve_step, 1)
                links[1] += 1
                dve.wait_ge(s_dve_step, links[0] + links[1])

            dve.sem_inc(s_y_out, CREDIT)
            dve.wait_ge(s_in_vec, 48)
            V.tensor_scalar(bq, bq, SCALE0, None, ALU.mult)
            link(V.tensor_scalar(gb2, gb2, RES, None, ALU.mult))

            def product_lo(i):
                dve.wait_ge(s_prod_hi, i + 1)
                for cols, factor in product_parts(i):
                    at = HALF * (i % KB)
                    stage = product_stage(i // KB)
                    last = V.scalar_tensor_tensor(stage[:, 2048 + at + cols.start:2048 + at + cols.stop],
                                                  big[i % 2][:, cols], factor,
                                                  stage[:, at + cols.start:at + cols.stop].bitcast(f32),
                                                  ALU.mult, ALU.subtract)
                last.then_inc(s_prod_lo, 1)

            for n, rows in ((1, range(8, 12)), (2, range(0, 8))):
                dve.wait_ge(s_norm_pow, n)
                cols = slice(rows.start, rows.stop)
                link(V.tensor_tensor(wscale[:, cols], rnorm[:, cols], g_l1[:, cols], ALU.mult))
                for j in rows:
                    V.tensor_scalar(w1_block(j), w1_block(j), wscale[:, j:j + 1], None, ALU.mult)\
                     .then_inc(s_w_normed, 1)
                if n == 1:
                    product_lo(0)
                    product_lo(1)
            product_lo(2)
            product_lo(3)
            dve.wait_ge(s_norm_pow, 3)
            link(V.tensor_tensor(wscale[:, 12:16], rnorm[:, 12:16], g_l1[:, 12:16], ALU.mult))
            link(V.tensor_scalar(wscale[:, 12:16], wscale[:, 12:16], RES, None, ALU.mult))
            for i, (w, src) in enumerate(((W[0], X[:, 0:2, :]), (W[1], X[:, 2:4, :]))):
                dve.wait_ge(s_split_hi, i + 1)
                V.tensor_tensor(w[:, 2048:4096], src.rearrange("p a n -> p (a n)"), w[:, 0:2048].bitcast(f32),
                                ALU.subtract).then_inc(s_split_lo, 1)
            for i in range(PAIRS):
                if i % 2 == 0:
                    product_lo(KB + i // 2)
                dve.wait_ge(s_split_hi, i + 3)
                for part, factor in ((0, SCALE0), (1, 1.0)):
                    last = V.scalar_tensor_tensor(qk_part_of(VT[:, 2 * i + 1, :], part),
                                                  qk_part_of(wqk_stage(i), part), factor,
                                                  qk_part_of(VT[:, 2 * i, :], part).bitcast(f32),
                                                  ALU.mult, ALU.subtract)
                last.then_inc(s_split_lo, 1)
            product_lo(KB + 2)
            product_lo(KB + 3)

            def channel_stats(k):
                V.bn_stats(stats[:, k, 0:6], XA[:, k, 0:HALF])
                link(V.bn_stats(stats[:, k, 6:12], XA[:, k, HALF:N]))
                own_wait(dve)
                return V.bn_aggr(mv[:, k, :], stats[:, k, :])

            def group_dev(tile, mean):
                link(V.tensor_tensor(dev, mean, tile[:, 0:KB], ALU.subtract))
                V.tensor_copy(gmean, tile[:, 0:KB])
                V.tensor_tensor(dev, dev, dev, ALU.mult).then_inc(s_gn_var, 1)

            def group_veps(tile):
                V.tensor_scalar(veps, tile[:, 0:KB], GN_EPS, None, ALU.add).then_inc(s_gn_veps, 1)

            def group_coef_a(n, scale):
                dve.wait_ge(s_gn_rstd, n)
                link(V.tensor_tensor(coefA, rstd, scale, ALU.mult))

            def group_coef_b(bias, times):
                link(V.scalar_tensor_tensor(coefT, gmean, times, coefA, ALU.mult, ALU.mult))
                return V.tensor_tensor(coefB, bias, coefT, ALU.subtract)

            def norm_f32():
                for k in range(KB):
                    V.tensor_scalar(XA[:, k, :], XA[:, k, :], coefA[:, k:k + 1], coefB[:, k:k + 1],
                                    ALU.mult, ALU.add).then_inc(s_hn_f, 1)

            def norm_lo(n):
                for k in range(KB):
                    dve.wait_ge(s_hn_hi, n * 4 + k + 1)
                    V.tensor_tensor(HL[:, k, :], XA[:, k, :], HH[:, k, :].bitcast(f32), ALU.subtract)\
                     .then_inc(s_hn_ready, 1)

            dve.wait_ge(s_x_next, 16)
            for k in range(KB):
                last = channel_stats(k)
            last.then_inc(s_gn_mean, 1)
            product_lo(2 * KB)
            dve.wait_ge(s_gn_mean, 1)
            dve.wait_ge(s_gn_first, 1)
            group_dev(ops[0], mv[:, :, 0])
            product_lo(2 * KB + 1)
            dve.wait_ge(s_gn_first, 2)
            group_veps(ops[1])
            group_coef_a(1, gs1)
            link(group_coef_b(gb1, 1.0))
            norm_f32()
            norm_lo(0)
            product_lo(2 * KB + 2)
            product_lo(2 * KB + 3)
            links_before = links[1]

            def body(b, last_batch):
                links[0], links[1] = links_before + b * DVE_LINKS, 0

                def at(key):
                    return big_count(b, key)

                def tile(key):
                    return big[big_at(b, key) % 2]

                def v_lo(i):
                    dve.wait_ge(s_big_hi, hi_count(b, ("v", i)))
                    v = v_heads(2 * i, 2 * i + 2)
                    V.tensor_tensor(v[:, :, 1:3, :], tile(("v", i))[:].rearrange("p (q x d) -> p q x d", x=2, d=CH),
                                    v[:, :, 0:4:3, :].bitcast(f32), ALU.subtract).then_inc(s_v_ready, 1)

                def last_v_lo(s):
                    dve.wait_ge(s_v_hi, b * 2 + s - 5)
                    v = v_heads(s, s + 1)
                    V.tensor_tensor(v[:, :, 1:3, :], ops[s % 2][:].rearrange("p (q x d) -> p q x d", x=2, d=CH),
                                    v[:, :, 0:4:3, :].bitcast(f32), ALU.subtract).then_inc(s_v_ready, 1)

                def qk_lo(j):
                    pair, what, half = j // 4, j % 4 // 2, j % 2
                    dve.wait_ge(s_big_hi, hi_count(b, ("qk", j)))
                    cols = slice(HALF * half, HALF * half + HALF)
                    V.scalar_tensor_tensor(unstacked(what, 1)[:, cols], tile(("qk", j))[:, 0:HALF],
                                           (bq, bk)[what][:, pair:pair + 1],
                                           unstacked(what, 0)[:, cols].bitcast(f32), ALU.add, ALU.subtract)\
                     .then_inc(s_nat_ready, 1)

                def row_max(u, tb):
                    i = 4 * (u % 2) + tb
                    dve.wait_ge(s_big_full, at(("s", 4 * u + tb)))
                    V.tensor_reduce(negmax[:, i:i + 1], tile(("s", 4 * u + tb))[:], axis=AX.X, op=ALU.max,
                                    negate=True).then_inc(s_row_max, 1)

                def recip(u, tb):
                    i = 4 * (u % 2) + tb
                    dve.wait_ge(s_exp_done, b * 72 + 4 * u + tb + 1)
                    V.reciprocal(rinv[:, i:i + 1], rowsum[:, i:i + 1]).then_inc(s_recip_done, 1)

                def pt_lo(u, s):
                    n = 8 * u + s
                    dve.wait_ge(s_pt_hi, b * 144 + n + 1)
                    V.tensor_tensor(pt_slot(u, s)[:, 1, :], tps[n % 2][:], pt_slot(u, s)[:, 0, :].bitcast(f32),
                                    ALU.subtract).then_inc(s_pt_ready, 1)

                for j in range(4):
                    qk_lo(j)
                for i in range(3):
                    v_lo(i)
                for step in range(STEPS0 + LAG):
                    u, tb, n = step // 4, step % 4, 2 * (step - LAG)
                    if qk_part(step) is not None:
                        qk_lo(qk_part(step))
                    if tb == 0 and 4 <= step <= STEPS0:
                        recip((step - 1) // 4, (step - 1) % 4)
                    if step < STEPS0:
                        row_max(u, tb)
                    if last_values(step - 1):
                        last_v_lo(last_values(step - 1))
                    if 1 <= step < STEPS0 and tb:
                        recip((step - 1) // 4, (step - 1) % 4)
                    if n >= 0:
                        pt_lo(n // 8, n % 8)
                        pt_lo(n // 8, n % 8 + 1)
                for half in range(2):
                    dve.wait_ge(s_a_hi, b * 8 + 7 + half)
                    cols = slice(HALF * half, HALF * half + HALF)
                    V.tensor_tensor(HL[:, 3, cols], XA[:, 3, cols], HH[:, 3, cols].bitcast(f32), ALU.subtract)\
                     .then_inc(s_a_lo_last, 1)

                for k in range(KB):
                    dve.wait_ge(s_proj_half, b * 4 + k + 1)
                    V.bn_stats(stats[:, k, 0:6], tile(("proj", k))[:, 0:HALF]).then_inc(s_pr_stats, 1)
                    dve.wait_ge(s_big_full, at(("proj", k)))
                    V.bn_stats(stats[:, k, 6:12], tile(("proj", k))[:, HALF:N]).then_inc(s_pr_stats, 1)
                    dve.wait_ge(s_pr_stats, b * 8 + 2 * k + 2)
                    own_wait(dve)
                    last = V.bn_aggr(mv[:, k, :], stats[:, k, :])
                last.then_inc(s_gn_mean, 1)
                dve.wait_ge(s_gn_mean, 2 * b + 2)
                link(V.tensor_tensor(cmean, mv[:, :, 0], bp, ALU.add))
                dve.wait_ge(s_big_full, at(("gna", 0)))
                group_dev(tile(("gna", 0)), cmean)
                dve.wait_ge(s_big_full, at(("gnb", 0)))
                group_veps(tile(("gnb", 0)))
                group_coef_a(2 * b + 2, gs2)
                group_coef_b(gb2, RES).then_inc(s_coef_b, 1)
                dve.wait_ge(s_x_res, b * 16 + 16)
                for i, (k, cols) in enumerate(XC_PARTS):
                    V.scalar_tensor_tensor(XA[:, k, cols], XA[:, k, cols], coefA[:, k:k + 1], X[:, k, cols],
                                           ALU.mult, ALU.add).then_inc(s_res_sum, 1)
                    for j in {2: (0, 1), 3: (2,), 4: (3,)}.get(i, ()):
                        xc_lo(b, j)

                for k in range(KB):
                    dve.wait_ge(s_big_full, at(("g", k)))
                    V.tensor_tensor(PB[:, 4 + k, :], tile(("g", k))[:], X[:, k, :], ALU.mult)\
                     .then_inc(s_prod_ready, 1)
                    if k == 0:
                        xc_lo(b, len(XC_PARTS) - 1)
                    if k:
                        dve.wait_ge(s_prod_ready, b * 4 + k + 1)
                        if k > 1:
                            dve.wait_ge(s_dve_step, links[0] + links[1])
                        total = V.tensor_tensor(PB[:, 4, :], PB[:, 4, :], PB[:, 4 + k, :], ALU.add)
                        if k < KB - 1:
                            total.then_inc(s_dve_step, 1)
                            links[1] += 1
                total.then_inc(s_prod_sum, 1)

                def y_lo(k):
                    dve.wait_ge(s_big_hi, hi_count(b, ("y", k)))
                    V.tensor_tensor(ST[:, 4 + k, :], tile(("y", k))[:], ST[:, k, :].bitcast(f32), ALU.subtract)\
                     .then_inc(s_y_ready, 1)

                def vp_lo(s):
                    dve.wait_ge(s_big_hi, hi_count(b, ("u", s)))
                    V.scalar_tensor_tensor(VT[:, s, HALF:N], tile(("u", s))[:, 0:HALF], rcol[:, s:s + 1],
                                           VT[:, s, 0:HALF].bitcast(f32), ALU.mult, ALU.subtract)\
                     .then_inc(s_vp_ready, 1)

                y_lo(0)
                y_lo(1)
                dve.wait_ge(s_sum_full, b + 1)
                V.tensor_scalar(mean_sq, ops[0][:, 0:8], 1.0 / (3 * C * RES * RES), 0.0, ALU.mult, ALU.max)\
                 .then_inc(s_ms_done, 1)
                dve.wait_ge(s_rms_done, b + 1)
                link(V.tensor_scalar(rms, rms, RMS_EPS, RES, ALU.add, ALU.mult))
                link(V.reciprocal(rcol, rms))
                for s in range(NT):
                    last = V.tensor_scalar(PB[:, 0, P * s:P * s + P], ident[:], rcol[:, s:s + 1], None, ALU.mult)
                last.then_inc(s_diag_ready, 1)
                y_lo(2)
                y_lo(3)
                for s in range(3):
                    vp_lo(s)
                dve.wait_ge(s_big_full, at(("r", 0)))
                V.tensor_copy(RB[:], tile(("r", 0))[:]).then_inc(s_r_ready, 1)
                for s in range(3, NT):
                    vp_lo(s)

                def scaled_max(i):
                    dve.wait_ge(s_big_full, at(("s1", i)))
                    if i == 0:
                        dve.wait_ge(s_r_ready, b + 1)
                    own_wait(dve)
                    V.tensor_tensor_reduce(out=PB[:, i, :], in0=tile(("s1", i))[:], in1=RB[:], scale=1.0,
                                           scalar=NEG, op0=ALU.mult, op1=ALU.max,
                                           accum_out=rowmax1[:, i:i + 1]).then_inc(s_s1_ready, 1)

                def recip1(i):
                    dve.wait_ge(s_exp_done, b * 72 + 64 + i + 1)
                    V.reciprocal(rinv[:, i:i + 1], rowsum[:, i:i + 1]).then_inc(s_recip_done, 1)

                def layer_out(j):
                    c, e = j // 4, j % 4
                    dve.wait_ge(s_o_full, b * 24 + UNITS0 + j + 1 + CREDIT)
                    xs = X[:, e, HALF * c:HALF * c + HALF]
                    V.scalar_tensor_tensor(xs, ops[j % 2][:], wscale[:, 12 + e:13 + e], xs, ALU.mult, ALU.add)\
                     .then_inc(s_y_out, 1)

                for i in range(4):
                    scaled_max(i)
                    if i:
                        recip1(i - 1)
                    if not last_batch:
                        if i == 0:
                            dve.wait_ge(s_x_next, (b + 2) * 16)
                        last = channel_stats(i)
                if not last_batch:
                    last.then_inc(s_gn_mean, 1)
                recip1(3)
                for tb in range(4):
                    scaled_max(4 + tb)
                    if not last_batch and tb == 2:
                        dve.wait_ge(s_gn_mean, 2 * b + 3)
                        dve.wait_ge(s_big_full, at(("gna", 1)))
                        group_dev(tile(("gna", 1)), mv[:, :, 0])
                    if not last_batch and tb == 3:
                        dve.wait_ge(s_big_full, at(("gnb", 1)))
                        group_veps(tile(("gnb", 1)))
                    pt_lo(UNITS0, 2 * tb)
                    pt_lo(UNITS0, 2 * tb + 1)
                    recip1(4 + tb)
                    if not last_batch and tb == 3:
                        group_coef_a(2 * b + 3, gs1)
                        group_coef_b(gb1, 1.0).then_inc(s_dve_step, 1)
                        links[1] += 1
                layer_out(0)
                layer_out(1)
                if not last_batch:
                    dve.wait_ge(s_dve_step, links[0] + links[1])
                    norm_f32()
                layer_out(2)
                if not last_batch:
                    norm_lo(b + 1)
                pt_lo(UNITS0 + 1, 0)
                pt_lo(UNITS0 + 1, 1)
                layer_out(3)
                for s in range(2, NT):
                    pt_lo(UNITS0 + 1, s)
                for j in range(4, 8):
                    layer_out(j)
                if not last_batch:
                    assert links[1] == DVE_LINKS, links[1]

            def xc_lo(b, i):
                k, cols = XC_PARTS[i]
                dve.wait_ge(s_xc_hi, b * len(XC_PARTS) + i + 1)
                dve.wait_ge(s_xc_ready, b * len(XC_PARTS) + i + 1)
                V.tensor_tensor(HL[:, k, cols], X[:, k, cols], HH[:, k, cols].bitcast(f32), ALU.subtract)\
                 .then_inc(s_xc_lo, 1)

            each_batch(dve, body)


NEG = -3.0e38


def kernel(**inputs):
    import numpy as np
    import concourse.bacc as bacc
    from concourse.bass_utils import run_bass_kernel_spmd

    nc = bacc.Bacc("TRN2", target_bir_lowering=False, num_devices=1, dynamic_dma_scratch_size=1024)
    g = {k: np.asarray(v) for k, v in inputs.items()}

    def blocks(w_t, cols):
        return np.ascontiguousarray(w_t.reshape(KB, P, cols).transpose(1, 0, 2).reshape(P, KB * cols))

    def columns(v):
        return v.reshape(-1, P).T

    w = g["L0_conv_w_qkv"].reshape(HEADS, 3, CH, C)
    bqkv = g["L0_conv_b_qkv"].reshape(HEADS, 3, CH)
    wqk = [blocks(np.concatenate([w[2 * p:2 * p + 2, j].reshape(P, C) for j in (0, 1)]).T, 2 * P) for p in range(PAIRS)]
    arrays = {
        "x": g["x"].reshape(B, C, N),
        "wv_t": blocks(w[:, 2].reshape(C, C).T, C),
        "wp_t": blocks(g["L0_conv_w_proj"].T, C),
        "wqk_t": np.stack(wqk),
        "v_qkv": g["L1_conv_v_qkv"].reshape(12, P, C),
        "v_out": blocks(g["L1_conv_v_out"], C),
        "wo_t": blocks(g["L1_conv_v_out"].T, C),
        "vecs": np.concatenate([columns(bqkv[:, j].reshape(C)) for j in range(3)]
                               + [columns(g[k]) for k in ("L0_conv_gn1_scale", "L0_conv_gn1_bias", "L0_conv_gn2_scale",
                                                          "L0_conv_gn2_bias", "L0_conv_b_proj", "L1_conv_g_qkv",
                                                          "L1_conv_g_out")], axis=1),
        "consts": np.stack([np.eye(P, dtype=np.float32),
                            np.kron(np.eye(P // 16), np.full((16, 16), 1 / 16)).astype(np.float32)]),
    }
    arrays = {f"in_{k}": np.ascontiguousarray(v) for k, v in arrays.items()}
    aps = [nc.dram_tensor(k, v.shape, f32, kind="ExternalInput").ap() for k, v in arrays.items()]
    out = nc.dram_tensor("out", (B, C, N), f32, kind="ExternalOutput").ap()
    build(nc, *aps, out)
    r = run_bass_kernel_spmd(nc, [arrays], core_ids=[0])
    return r.results[0]["out"].reshape(B, C, 32, 32)
```
